# Optimizing a Trainium2 kernel written in Bass

```python
import numpy as np
import jax
import jax.numpy as jnp

def _softmax(x, axis=-1):
    return jax.nn.softmax(x, axis=axis)

def _gelu(x):
    return jax.nn.gelu(x, approximate=True)

def _silu(x):
    return jax.nn.silu(x)

def _sigmoid(x):
    return jax.nn.sigmoid(x)

def _layernorm(x, axis=-1, eps=1e-05):
    m = jnp.mean(x, axis=axis, keepdims=True)
    v = jnp.var(x, axis=axis, keepdims=True)
    return (x - m) / jnp.sqrt(v + eps)

def _scatter_add(tgt, idx, src, axis=0):
    return tgt.at[idx].add(src)

def _segment_sum(src, seg, n):
    return jax.ops.segment_sum(src, seg, n)
kernel_name = 'mk_seq_postln_d1_jaxref_r4_1a6f00'

def setup_inputs(seed: int=0):
    np.random.seed(seed)
    _w = jnp.asarray

    def _L0_attn_setup():
        import jax, jax.numpy as jnp
        import numpy as np
        DIM = 256
        HEADS = 1
        HDIM = DIM // HEADS
        INNER = 16
        B, L = (2, 1024)
        ROPE_BASE = 32.0

        def _apply_rope(x, pos, base):
            d = x.shape[-1]
            inv_freq = base ** (-jnp.arange(0, d, 2, dtype=jnp.float32) / d)
            ang = pos[:, None].astype(jnp.float32) * inv_freq
            emb = jnp.concatenate([ang, ang], axis=-1)
            cos = jnp.cos(emb)[None, :, None, :].astype(x.dtype)
            sin = jnp.sin(emb)[None, :, None, :].astype(x.dtype)
            x1, x2 = (x[..., :d // 2], x[..., d // 2:])
            rot = jnp.concatenate([-x2, x1], axis=-1)
            return x * cos + rot * sin
        key = jax.random.key(seed)
        ks = jax.random.split(key, 7)
        hidden_states = jax.random.normal(ks[0], (B, L, DIM), dtype=jnp.float32)
        Wq = jax.random.normal(ks[1], (DIM, DIM), dtype=jnp.float32) * 0.02
        Wk = jax.random.normal(ks[2], (DIM, DIM), dtype=jnp.float32) * 0.02
        fc1_w = jax.random.normal(ks[3], (INNER, 1), dtype=jnp.float32) * 0.1
        fc1_b = jax.random.normal(ks[4], (INNER,), dtype=jnp.float32) * 0.1
        fc2_w = jax.random.normal(ks[5], (DIM, INNER), dtype=jnp.float32) * 0.1
        fc2_b = jax.random.normal(ks[6], (DIM,), dtype=jnp.float32) * 0.1
        return {'hidden_states': hidden_states, 'Wq': Wq, 'Wk': Wk, 'fc1_w': fc1_w, 'fc1_b': fc1_b, 'fc2_w': fc2_w, 'fc2_b': fc2_b}
    _L0_attn_in = _L0_attn_setup()

    def _L0_ffn_setup():
        import jax, jax.numpy as jnp
        import numpy as np
        TAU = 1.0
        K_ROUTE = 3
        EPS = 1e-08

        def _route_combine_weights(x_addr, U, k, tau):
            z = x_addr @ U.T
            topv, topi = jax.lax.top_k(z, k)
            w = jax.nn.softmax(topv / (tau + EPS), axis=1)
            N, L = z.shape
            rows = jnp.arange(N)[:, None]
            return jnp.zeros((N, L), z.dtype).at[rows, topi].add(w)

        def _mixture(inp, C, W):
            L = W.shape[0]
            y = jnp.zeros((inp.shape[0], W.shape[1]), inp.dtype)
            for e in range(L):
                y = y + C[:, e:e + 1] * (inp @ W[e].T)
            return y
        key = jax.random.key(seed)
        ks = jax.random.split(key, 8)
        B, T, D_in, H, D_out, L, d_addr = (8, 2048, 256, 256, 256, 12, 64)

        def unit_rows(k, L_, d_):
            U = jax.random.normal(k, (L_, d_), dtype=jnp.float32)
            U = U - U.mean(axis=1, keepdims=True)
            return U / (jnp.linalg.norm(U, axis=1, keepdims=True) + EPS)

        def norm_tape(k, shape):
            W = jax.random.normal(k, shape, dtype=jnp.float32)
            n = jnp.sqrt(jnp.sum(W * W, axis=tuple(range(1, W.ndim)), keepdims=True)) + 1e-12
            return W / n
        x = jax.random.normal(ks[0], (B, T, D_in), dtype=jnp.float32)
        P_w = jax.random.normal(ks[1], (d_addr, D_in), dtype=jnp.float32) / np.sqrt(D_in)
        U1 = unit_rows(ks[2], L, d_addr)
        U2 = unit_rows(ks[3], L, d_addr)
        U3 = unit_rows(ks[4], L, d_addr)
        W1 = norm_tape(ks[5], (L, H, D_in))
        W2 = norm_tape(ks[6], (L, D_out, H))
        b2 = norm_tape(ks[7], (L, D_out))
        return {'x': x, 'P_w': P_w, 'U1': U1, 'U2': U2, 'U3': U3, 'W1': W1, 'W2': W2, 'b2': b2}
    _L0_ffn_in = _L0_ffn_setup()
    _d = {'L0_attn_hidden_states': _L0_attn_in['hidden_states'], 'L0_attn_Wq': _L0_attn_in['Wq'], 'L0_attn_Wk': _L0_attn_in['Wk'], 'L0_attn_fc1_w': _L0_attn_in['fc1_w'], 'L0_attn_fc1_b': _L0_attn_in['fc1_b'], 'L0_attn_fc2_w': _L0_attn_in['fc2_w'], 'L0_attn_fc2_b': _L0_attn_in['fc2_b'], 'L0_ffn_P_w': _L0_ffn_in['P_w'], 'L0_ffn_U1': _L0_ffn_in['U1'], 'L0_ffn_U2': _L0_ffn_in['U2'], 'L0_ffn_U3': _L0_ffn_in['U3'], 'L0_ffn_W1': _L0_ffn_in['W1'], 'L0_ffn_W2': _L0_ffn_in['W2'], 'L0_ffn_b2': _L0_ffn_in['b2']}
    _x0 = _d['L0_attn_hidden_states']
    _d['L0_attn_hidden_states'] = jax.random.normal(jax.random.fold_in(jax.random.key(seed), 1), (8, 512, 256), dtype=_x0.dtype)
    del _x0
    return _d

def reference(L0_attn_hidden_states, L0_attn_Wq, L0_attn_Wk, L0_attn_fc1_w, L0_attn_fc1_b, L0_attn_fc2_w, L0_attn_fc2_b, L0_ffn_P_w, L0_ffn_U1, L0_ffn_U2, L0_ffn_U3, L0_ffn_W1, L0_ffn_W2, L0_ffn_b2):

    def _L0_attn_ref(hidden_states, Wq, Wk, fc1_w, fc1_b, fc2_w, fc2_b):
        import jax, jax.numpy as jnp
        import numpy as np
        DIM = 256
        HEADS = 1
        HDIM = DIM // HEADS
        INNER = 16
        B, L = (2, 1024)
        ROPE_BASE = 32.0

        def _apply_rope(x, pos, base):
            d = x.shape[-1]
            inv_freq = base ** (-jnp.arange(0, d, 2, dtype=jnp.float32) / d)
            ang = pos[:, None].astype(jnp.float32) * inv_freq
            emb = jnp.concatenate([ang, ang], axis=-1)
            cos = jnp.cos(emb)[None, :, None, :].astype(x.dtype)
            sin = jnp.sin(emb)[None, :, None, :].astype(x.dtype)
            x1, x2 = (x[..., :d // 2], x[..., d // 2:])
            rot = jnp.concatenate([-x2, x1], axis=-1)
            return x * cos + rot * sin
        b, l, _ = hidden_states.shape
        q = (hidden_states @ Wq.T).reshape(b, l, HEADS, HDIM).astype(jnp.bfloat16)
        k = (hidden_states @ Wk.T).reshape(b, l, HEADS, HDIM).astype(jnp.bfloat16)
        pos = jnp.arange(l)
        q = _apply_rope(q, pos, ROPE_BASE)
        k = _apply_rope(k, pos, ROPE_BASE)
        scores = jnp.einsum('bqhd,bkhd->bhqk', q.astype(jnp.float32), k.astype(jnp.float32)) / HDIM ** 0.5
        causal = jnp.tril(jnp.ones((l, l), dtype=bool))
        exp_qk = jnp.where(causal[None, None], jnp.exp(scores), 0.0)
        o = jnp.swapaxes(exp_qk.sum(axis=-1), 1, 2)
        o = jax.nn.relu(o @ fc1_w.T + fc1_b)
        return o @ fc2_w.T + fc2_b

    def _L0_ffn_ref(x, P_w, U1, U2, U3, W1, W2, b2):
        import jax, jax.numpy as jnp
        import numpy as np
        TAU = 1.0
        K_ROUTE = 3
        EPS = 1e-08

        def _route_combine_weights(x_addr, U, k, tau):
            z = x_addr @ U.T
            topv, topi = jax.lax.top_k(z, k)
            w = jax.nn.softmax(topv / (tau + EPS), axis=1)
            N, L = z.shape
            rows = jnp.arange(N)[:, None]
            return jnp.zeros((N, L), z.dtype).at[rows, topi].add(w)

        def _mixture(inp, C, W):
            L = W.shape[0]
            y = jnp.zeros((inp.shape[0], W.shape[1]), inp.dtype)
            for e in range(L):
                y = y + C[:, e:e + 1] * (inp @ W[e].T)
            return y
        B, T, D = x.shape
        xf = x.reshape(B * T, D)
        xa = xf @ P_w.T
        C1 = _route_combine_weights(xa, U1, K_ROUTE, TAU)
        C2 = _route_combine_weights(xa, U2, K_ROUTE, TAU)
        C3 = _route_combine_weights(xa, U3, K_ROUTE, TAU)
        h = jax.nn.gelu(_mixture(xf, C1, W1), approximate=False)
        y = _mixture(h, C2, W2) + C3 @ b2
        return y.reshape(B, T, -1)
    x = L0_attn_hidden_states
    x = _layernorm(x + _L0_attn_ref(x, L0_attn_Wq, L0_attn_Wk, L0_attn_fc1_w, L0_attn_fc1_b, L0_attn_fc2_w, L0_attn_fc2_b), axis=-1)
    x = _layernorm(x + _L0_ffn_ref(x, L0_ffn_P_w, L0_ffn_U1, L0_ffn_U2, L0_ffn_U3, L0_ffn_W1, L0_ffn_W2, L0_ffn_b2), axis=-1)
    return x

_drawn_inputs = setup_inputs


def setup_inputs(seed=0):
    import zlib

    import numpy as np

    out = dict(_drawn_inputs(seed))
    spreads = {}
    factors = {'L0_attn_Wq': 8.0,
     'L0_attn_Wk': 8.0,
     'L0_attn_fc1_b': 26.051,
     'L0_ffn_U1': 8.0,
     'L0_ffn_U2': 8.0,
     'L0_ffn_W1': 8.0,
     'L0_ffn_W2': 8.0,
     'L0_attn_fc2_b': 7.102}
    for name, (base, spread) in spreads.items():
        noise = np.random.default_rng([zlib.crc32(name.encode()), seed]).standard_normal(out[name].shape)
        drawn = base * np.exp(spread * noise) if base else spread * noise
        out[name] = jnp.asarray(drawn.astype(out[name].dtype))
    for name, factor in factors.items():
        out[name] = (out[name] * factor).astype(out[name].dtype)
    return out
```

```python
from contextlib import ExitStack

import numpy as np

import concourse.bass as bass
from concourse import mybir

ALU = mybir.AluOpType
ACT = mybir.ActivationFunctionType
AX = mybir.AxisListType
ENGINE = mybir.EngineType
F32 = mybir.dt.float32
F16 = mybir.dt.float16
BF16 = mybir.dt.bfloat16
I32 = mybir.dt.int32
U32 = mybir.dt.uint32

P = 128
DIM = 256
NC = DIM // P
NSEQ, SEQ = 8, 512
TPS = SEQ // P
NT = NSEQ * TPS
INNER = 16
PAD = 32
NE = 12
NS = NE + 1
TOPK = 3
NR = 3
NM = 2
REC = 4
NREC = NE // TOPK
GROUPS = TPS * NM
EPS = 1e-5
MASKED = -1e30
ROPE_BASE = 32.0

C_COS, C_SIN = 0, SEQ
C_IDENT = 2 * SEQ
C_MASK = C_IDENT + P
C_TRI = C_MASK + P
C_PICK = C_TRI + GROUPS * NE
C_EVEC = C_PICK + GROUPS * NREC * REC
C_ONES = C_EVEC + 1
NCONST = C_ONES + 1


def shape_constants():
    half = DIM // 2
    inv = np.float32(ROPE_BASE) ** (-np.arange(0, DIM, 2, dtype=np.float32) / np.float32(DIM))
    ang = np.arange(SEQ, dtype=np.float32)[:, None] * inv.astype(np.float32)
    c = np.zeros((P, NCONST), np.float32)
    assert half == P
    c[:, C_COS:C_COS + SEQ] = np.cos(ang).T
    c[:, C_SIN:C_SIN + SEQ] = np.sin(ang).T
    c[:, C_IDENT:C_IDENT + P] = np.eye(P)
    q, k = np.arange(P)[:, None], np.arange(P)[None, :]
    c[:, C_MASK:C_MASK + P] = np.where(k > q, MASKED, 0.0)
    n = GROUPS * NE
    i, j = np.arange(n)[:, None], np.arange(n)[None, :]
    c[:n, C_TRI:C_TRI + n] = (i // NE == j // NE) & (i <= j)
    place = np.array([[g * TOPK + r + 1 for r in range(REC)] for g in range(NREC)]).reshape(-1)
    place[place > NE] = -1
    for g in range(GROUPS):
        c[:n, C_PICK + g * NREC * REC:C_PICK + (g + 1) * NREC * REC] = -1
        c[g * NE:(g + 1) * NE, C_PICK + g * NREC * REC:C_PICK + (g + 1) * NREC * REC] = place
    c[:n, C_EVEC] = np.arange(n) % NE + 1
    c[:, C_ONES] = 1
    return c


def build(nc, x, xT, wqkT, gate, fc2, p_w, uT, w1T, w2T, b2e, constb, constf, out):
    ctx = ExitStack()
    with ctx:
        def sb(name, shape, dt):
            return ctx.enter_context(nc.sbuf_tensor(name, shape, dt))

        def ps(name, shape, dt=F32):
            return ctx.enter_context(nc.psum_tensor(name, shape, dt))

        def sem(name):
            return ctx.enter_context(nc.semaphore(name))

        xs = sb("xs", [P, NT, DIM], F32)
        x1 = sb("x1", [P, TPS, DIM], F32)
        x1T = sb("x1T", [P, NT, 2, NC, P], F16)
        W = sb("W", [P, NM, NS, 2, NC * DIM], F16)
        xTb = sb("xTb", [P, 2, NC, SEQ], F32)
        wqk = sb("wqk", [P, NC, 4, P], F32)
        cb = sb("cb", [P, NCONST], BF16)
        identf = sb("identf", [P, P], F32)
        iota12 = sb("iota12", [P, NE], F32)
        gatew = sb("gatew", [P, 2, PAD], F32)
        fc2s = sb("fc2s", [P, DIM], F32)
        b2s = sb("b2s", [P, DIM], F32)
        pws = sb("pws", [64, NC, P], F32)
        uTs = sb("uTs", [64, NR * NE], F32)
        MT = sb("MT", [P, 2, NC, NR * NE], F16)
        MTf = sb("MTf", [P, NC, NR * NE], F32)
        qk = sb("qk", [P, 2, NC, SEQ], BF16)
        xcos = sb("xcos", [P, 2, NC, SEQ], BF16)
        xsin = sb("xsin", [P, 2, NC, SEQ], BF16)
        qkr = sb("qkr", [P, 2, NC, SEQ], BF16)
        expd = sb("expd", [P, 2, SEQ], BF16)
        o = sb("o", [P, 2, TPS], F32)
        hg = sb("hg", [P, TPS, PAD], F32)
        hgT = sb("hgT", [P, P], F32)
        stats = sb("stats", [P, TPS, 6], F32)
        mv = sb("mv", [P, TPS, 2], F32)
        ve = sb("ve", [P, TPS], F32)
        rstd = sb("rstd", [P, TPS], F32)
        minus_half = sb("minus_half", [P, TPS], F32)
        zs = sb("zs", [P, TPS * NR, NE], F32)
        top8 = sb("top8", [P, TPS * NR, 8], F32)
        idx8 = sb("idx8", [P, TPS * NR, 8], U32)
        ez = sb("ez", [P, TPS * NR, NE], F32)
        ez2 = sb("ez2", [P, TPS * NR, NE], F32)
        picked = sb("picked", [P, 3, TPS * NR, NE], F32)
        maskf = sb("maskf", [P, TPS * NR, NE], F32)
        maskb = sb("maskb", [P, TPS, NM, NE], BF16)
        esum = sb("esum", [P, TPS, NR], F32)
        escale = sb("escale", [P, TPS, NR], F32)
        C = sb("C", [P, NT, NM, NS], F32)
        C3 = sb("C3", [P, TPS, PAD], F32)
        C3T = sb("C3T", [P, P], F32)
        used = sb("used", [GROUPS * NE, 1], F32)
        usedb = sb("usedb", [GROUPS * NE, 1], BF16)
        rank = sb("rank", [GROUPS * NE, 1], F32)
        onehot = sb("onehot", [GROUPS * NE, GROUPS * NREC * REC], BF16)
        ids = sb("ids", [1, NT, NM, NREC, REC], I32)
        wtmp = sb("wtmp", [P, 2, NC * DIM], F32)
        amax = sb("amax", [P, 3], F32)
        amaxa = sb("amaxa", [P, 3], F32)
        pow2 = sb("pow2", [P, 3], F32)
        ipow2 = sb("ipow2", [P, 3], F32)
        scale = sb("scale", [P, 3], F32)
        iscale = sb("iscale", [P, 3], F32)
        cscale = sb("cscale", [P, NR], F32)
        acc1 = sb("acc1", [P, 2, DIM], F32)
        hact = sb("hact", [P, 2, DIM], F32)
        hT = sb("hT", [P, 2, 2, NC, P], F16)
        st2 = sb("st2", [P, 2, 6], F32)
        mv2 = sb("mv2", [P, 2, 2], F32)
        ve2 = sb("ve2", [P, 2], F32)
        rstd2 = sb("rstd2", [P, 2], F32)

        bank = [ps(f"bank{i}", [P, 512]) for i in range(8)]
        PROJ, SCORE, ROW, XPOSE, MISC = (0, 1), (2, 3), (4, 5), 6, 7
        MIX1, MIX2, EXTRA, HT = (0, 1), (2, 3), (4, 5), 6

        ld_const = sem("ld_const")
        ld_seq = sem("ld_seq")
        ld_w = sem("ld_w")
        proj_done = sem("proj_done")
        qk_copied = sem("qk_copied")
        rope_done = sem("rope_done")
        score_done = sem("score_done")
        exp_done = sem("exp_done")
        hg_done = sem("hg_done")
        hgT_done = sem("hgT_done")
        hgT_copied = sem("hgT_copied")
        row_done = sem("row_done")
        row_free = sem("row_free")
        mv_done = sem("mv_done")
        rstd_done = sem("rstd_done")
        x1_done = sem("x1_done")
        x1T_done = sem("x1T_done")
        x1hi_done = sem("x1hi_done")
        x1lo_done = sem("x1lo_done")
        z_done = sem("z_done")
        z_copied = sem("z_copied")
        ez_in = sem("ez_in")
        ez_done = sem("ez_done")
        mask_done = sem("mask_done")
        count_done = sem("count_done")
        used_done = sem("used_done")
        rank_done = sem("rank_done")
        onehot_done = sem("onehot_done")
        id_done = sem("id_done")
        ids_done = sem("ids_done")
        C3_done = sem("C3_done")
        C3T_done = sem("C3T_done")
        C3T_copied = sem("C3T_copied")
        C_done = sem("C_done")
        xres_done = sem("xres_done")
        M_done = sem("M_done")
        MT_done = sem("MT_done")
        amax_done = sem("amax_done")
        amaxa_done = sem("amaxa_done")
        scale_done = sem("scale_done")
        w_split = sem("w_split")
        zero_done = sem("zero_done")
        dve_attn = sem("dve_attn")
        dve_route = sem("dve_route")
        dve_setup = sem("dve_setup")
        dve_ffn = sem("dve_ffn")
        pool_step = sem("pool_step")
        m1_done = sem("m1_done")
        m1_init = sem("m1_init")
        m1_free = sem("m1_free")
        m2_done = sem("m2_done")
        m2_free = sem("m2_free")
        ex_done = sem("ex_done")
        ex_free = sem("ex_free")
        gelu_done = sem("gelu_done")
        hT_done = sem("hT_done")
        hhi_done = sem("hhi_done")
        hlo_done = sem("hlo_done")
        mv2_done = sem("mv2_done")
        rstd2_done = sem("rstd2_done")
        y_done = sem("y_done")
        stored = sem("stored")
        held = sem("held")

        Wf = W.rearrange("p m e h n -> p (m e) (h n)").bitcast(F32)

        def const(col, n, rows=P):
            return cb[0:rows, col:col + n]

        def wait(eng, s, value):
            if not (isinstance(value, int) and value <= 0):
                eng.wait_ge(s, value)

        def hold(eng, s, value):
            eng.wait_ge(s, value)
            if not isinstance(value, int):
                eng.sem_inc(held, 1)

        def by_sequence(step):
            def run(eng):
                step(0, True, False)
                with eng.Fori(1, NSEQ) as b:
                    step(b, True, True)
                step(NSEQ, False, True)
            return run

        def by_tile(eng, step):
            step(0, 0, True, False, False)
            step(1, 1, True, True, False)
            with eng.Fori(1, NT // 2) as pair:
                step(2 * pair, 0, True, True, True)
                step(2 * pair + 1, 1, True, True, True)
            step(NT, 0, False, True, True)
            step(NT + 1, 1, False, False, True)

        def load_ids(eng, engine, t, m, g):
            _, v = nc.values_load_multi_w_load_instructions(
                ids[0:1, bass.ds(t, 1), m, bass.ds(g, 1), :].rearrange("p a b c -> p (a b c)"),
                engines=[engine], min_val=0, max_val=NE,
                skip_runtime_bounds_check_because="an id is a sum of one-hot entries times 1..12")
            return v

        block = ctx.enter_context(nc.Block())

        @block.sync
        def _(sp):
            def load_seq(b):
                wait(sp, proj_done, 4 * (b - 1) if not isinstance(b, int) or b > 1 else 0)
                parity = b % 2
                sp.dma_start(xTb[:, bass.ds(parity, 1), :, :].rearrange("p a c n -> p (a c) n"),
                             xT[bass.ds(b, 1), :, :, :].rearrange("a p c n -> p (a c) n")).then_inc(ld_seq, 16)
                sp.dma_start(xs[:, bass.ds(b * TPS, TPS), :],
                             x[bass.ds(b, 1), :, :, :].rearrange("a t p d -> p (a t) d")).then_inc(ld_seq, 16)

            load_seq(0)
            sp.dma_start(pws[:, :, :], p_w.rearrange("k (c p) -> k c p", c=NC)).then_inc(ld_const, 16)
            sp.dma_start(uTs[:, :], uT).then_inc(ld_const, 16)
            sp.dma_start(fc2s[:, :], fc2).then_inc(ld_const, 16)
            sp.dma_start(b2s[:, :], b2e).then_inc(ld_const, 16)
            sp.wait_ge(ld_seq, 32)
            load_seq(1)
            for m, w in ((0, w1T), (1, w2T)):
                sp.dma_start(Wf[:, m * NS + 1:(m + 1) * NS, :], w.rearrange("p e n -> p e n")).then_inc(ld_w, 16)
                sp.wait_ge(ld_w, 16 * (m + 1))
            with sp.Fori(2, NSEQ) as b:
                sp.wait_ge(ld_seq, 32 * b)
                load_seq(b)
            with sp.Fori(0, NT) as t:
                sp.wait_ge(y_done, t + 1)
                sp.dma_start(out[bass.ds(t, 1), :, :].rearrange("a p d -> p (a d)"),
                             xs[:, bass.ds(t, 1), :].rearrange("p a d -> p (a d)")).then_inc(stored, 16)
            sp.wait_ge(stored, 16 * NT)

        @block.gpsimd
        def _(pool):
            steps = [0]

            def link(ins):
                steps[0] += 1
                ins.then_inc(pool_step, 1)
                pool.wait_ge(pool_step, steps[0])

            pool.memset(minus_half[:, :], -0.5).then_inc(zero_done, 1)
            pool.memset(C[:, :, :, 0:1], 0.0).then_inc(zero_done, 1)
            pool.memset(C3[:, :, :], 0.0).then_inc(zero_done, 1)
            for m in range(NM):
                pool.memset(Wf[:, m * NS, :], 0.0).then_inc(zero_done, 1)
            pool.wait_ge(zero_done, 5)
            pool.wait_ge(amax_done, 3)
            pool.partition_all_reduce(amaxa[:, :], amax[:, :], P, bass.bass_isa.ReduceOp.max).then_inc(amaxa_done, 1)
            pool.wait_ge(scale_done, 1)
            pieces = [(m, e) for m in range(NM) for e in range(1, NS)]
            per = len(pieces) // NSEQ
            for s in range(NSEQ):
                pool.wait_ge(mv_done, TPS * (s + 1))
                if s:
                    pool.wait_ge(x1_done, TPS * s)
                link(pool.tensor_scalar(ve[:, :], mv[:, :, 1], EPS, 0.0, ALU.add, ALU.add))
                pool.tensor_tensor(rstd[:, :], ve[:, :], minus_half[:, :], ALU.pow).then_inc(rstd_done, 1)
                for i, (m, e) in enumerate(pieces[s * per:(s + 1) * per]):
                    tmp = wtmp[:, i % 2, :]
                    link(pool.tensor_scalar(tmp, Wf[:, m * NS + e, :], scale[:, m:m + 1], 0.0, ALU.mult, ALU.add))
                    link(pool.tensor_copy(W[:, m, e, 0, :], tmp))
                    pool.tensor_tensor(W[:, m, e, 1, :], tmp, W[:, m, e, 0, :], ALU.subtract).then_inc(w_split, 1)
            base = steps[0]
            with pool.Fori(0, NT, 2) as t:
                for p in range(2):
                    hold(pool, mv2_done, t + p + 1)
                    pool.tensor_scalar(ve2[:, p:p + 1], mv2[:, p, 1:2], EPS, 0.0, ALU.add, ALU.add)\
                        .then_inc(pool_step, 1)
                    pool.wait_ge(pool_step, t + (base + p + 1))
                    pool.tensor_tensor(rstd2[:, p:p + 1], ve2[:, p:p + 1], minus_half[:, 0:1], ALU.pow)\
                        .then_inc(rstd2_done, 1)

        @block.scalar
        def _(act):
            act.dma_start(wqk[:, :, :, :], wqkT).then_inc(ld_const, 16)
            act.dma_start(cb[:, :], constb).then_inc(ld_const, 16)
            act.dma_start(identf[:, :], constf[:, 0:P]).then_inc(ld_const, 16)
            act.dma_start(iota12[:, :], constf[:, P:P + NE]).then_inc(ld_const, 16)
            act.dma_start(gatew[:, :, :], gate).then_inc(ld_const, 16)

            def step(b, attend, route):
                s = b - 1
                if route:
                    act.wait_ge(hgT_done, s + 1)
                    act.activation(hgT[:, :], bank[MISC][:, 0:P], ACT.Copy).then_inc(hgT_copied, 1)
                if attend:
                    if not isinstance(b, int):
                        act.wait_ge(rope_done, b)
                    for g in range(4):
                        act.wait_ge(proj_done, 4 * b + (g + 1))
                        act.activation(qk[:, g // 2, g % 2, :], bank[PROJ[g % 2]][:, :], ACT.Copy)\
                            .then_inc(qk_copied, 1)
                if route:
                    for t in range(TPS):
                        act.wait_ge(x1T_done, TPS * s + (t + 1))
                        act.activation(x1T[:, bass.ds(TPS * s + t, 1), 0, :, :].rearrange("p a c n -> p (a c n)"),
                                       bank[XPOSE][:, 0:DIM], ACT.Copy).then_inc(x1hi_done, 1)
                if attend:
                    if isinstance(b, int):
                        parity = b % 2
                    else:
                        parity = b % 2
                        act.wait_ge(hg_done, b)
                    for t in range(TPS):
                        act.wait_ge(score_done, TPS * b + (t + 1))
                        n = (t + 1) * P
                        act.activation(expd[:, t % 2, 0:n], bank[SCORE[t % 2]][:, 0:n], ACT.Exp, scale=float(DIM) ** -0.5,
                                       accum_out=o[:, bass.ds(parity, 1), t]).then_inc(exp_done, 1)
                if route:
                    act.wait_ge(ez_in, s + 1)
                    act.activation(ez2[:, :, :], ez[:, :, :], ACT.Exp).then_inc(ez_done, 1)
                    act.wait_ge(C3T_done, s + 1)
                    act.activation(C3T[:, :], bank[MISC][:, 0:P], ACT.Copy).then_inc(C3T_copied, 1)

            by_sequence(step)(act)

            def ffn(t, p, first, second, third):
                if second:
                    act.wait_ge(hT_done, t)
                    act.activation(hT[:, 1 - p, 0, :, :].rearrange("p c n -> p (c n)"), bank[HT][:, 0:DIM], ACT.Copy,
                                   scale=ipow2[:, 0:1]).then_inc(hhi_done, 1)
                if first:
                    v = load_ids(act, ENGINE.Activation, t, 0, 0)
                    act.wait_ge(m1_done, TOPK * t + 1)
                    b = MIX1[(TOPK * p) % 2]
                    act.activation(acc1[:, p, :], bank[b][:, 0:DIM], ACT.Copy,
                                   scale=C[:, bass.ds(t, 1), 0, bass.ds(v[0], 1)].rearrange("p a b -> p (a b)"))\
                        .then_inc(m1_init, 1)
                    act.wait_ge(m1_free, 2 * t + 4)
                    act.activation(hact[:, p, :], acc1[:, p, :], ACT.Gelu).then_inc(gelu_done, 1)

            act.wait_ge(ids_done, NSEQ)
            act.wait_ge(C_done, NSEQ)
            by_tile(act, ffn)

        @block.tensor
        def _(pe):
            pe.wait_ge(ld_const, 16 * 9)
            pe.wait_ge(ld_seq, 32)

            def step(b, attend, route):
                s = b - 1

                def project(g):
                    if g == 0:
                        pe.wait_ge(ld_seq, 32 * b + 32)
                    if not (isinstance(b, int) and g < 2):
                        pe.wait_ge(qk_copied, 4 * b + (g - 1))
                    for c in range(NC):
                        mm = pe.matmul(bank[PROJ[g % 2]][:, :], wqk[:, c, g, :],
                                       xTb[:, bass.ds(b % 2, 1), c, :].rearrange("p a n -> p (a n)"),
                                       start=(c == 0), stop=(c == NC - 1))
                    mm.then_inc(proj_done, 1)

                def rows(n, lhsT, rhs, t):
                    pe.wait_ge(row_free, n + 1)
                    lo, hi = PAD * t, PAD * (t + 1)
                    pe.matmul(bank[ROW[t % 2]][:, 0:DIM], lhsT[lo:hi, :], rhs[lo:hi, :],
                              start=True, stop=True).then_inc(row_done, 1)

                if route:
                    pe.wait_ge(hg_done, s + 1)
                    pe.wait_ge(C3T_copied, s + 1)
                    pe.transpose(bank[MISC][:, 0:P], hg[:, :, :].rearrange("p t n -> p (t n)"), identf[:, :])\
                        .then_inc(hgT_done, 1)
                if attend:
                    project(0)
                if route:
                    pe.wait_ge(hgT_copied, s + 1)
                    for t in (0, 1):
                        rows(2 * TPS * s + t, hgT, fc2s, t)
                if attend:
                    project(1)
                if route:
                    for t in (2, 3):
                        rows(2 * TPS * s + t, hgT, fc2s, t)
                if attend:
                    project(2)
                    project(3)
                if route:
                    for t in range(TPS):
                        pe.wait_ge(x1_done, TPS * s + (t + 1))
                        pe.wait_ge(x1lo_done, TPS * s + (t + 1))
                        for c in range(NC):
                            tr = pe.transpose(bank[XPOSE][:, c * P:(c + 1) * P],
                                              x1[:, t, c * P:(c + 1) * P], identf[:, :])
                        tr.then_inc(x1T_done, 1)
                if attend:
                    pe.wait_ge(rope_done, b + 1)
                    for t in range(TPS):
                        if not (isinstance(b, int) and t < 2):
                            pe.wait_ge(exp_done, TPS * b + (t - 1))
                        n = (t + 1) * P
                        sc = bank[SCORE[t % 2]]
                        for c in range(NC):
                            pe.matmul(sc[:, 0:n], qkr[:, 0, c, t * P:(t + 1) * P], qkr[:, 1, c, 0:n],
                                      start=(c == 0), stop=False, skip_group_check=True)
                        pe.matmul(sc[:, t * P:n], const(C_IDENT, P), const(C_MASK, P),
                                  start=False, stop=True, skip_group_check=True).then_inc(score_done, 1)
                if route:
                    pe.wait_ge(MT_done, 1)
                    pe.wait_ge(x1lo_done, TPS * s + (TPS + 1))
                    for t in range(TPS):
                        zr = bank[MISC][:, 128 + t * NR * NE:128 + (t + 1) * NR * NE]
                        k = 0
                        for c in range(NC):
                            for hx, hm in ((0, 0), (0, 1), (1, 0)):
                                mm = pe.matmul(zr, x1T[:, bass.ds(TPS * s + t, 1), hx, c, :].rearrange("p a n -> p (a n)"),
                                               MT[:, hm, c, :], start=(k == 0), stop=(k == 5))
                                k += 1
                    mm.then_inc(z_done, 1)
                    n = GROUPS * NE
                    pe.wait_ge(mask_done, s + 1)
                    pe.matmul(bank[MISC][0:n, 0:1], maskb[:, :, :, :].rearrange("p t m e -> p (t m e)"),
                              const(C_ONES, 1), start=True, stop=True).then_inc(count_done, 1)
                    pe.wait_ge(used_done, s + 1)
                    pe.matmul(bank[MISC][0:n, 0:1], const(C_TRI, n, n), usedb[:, :], start=True, stop=True)\
                        .then_inc(rank_done, 1)
                    pe.wait_ge(onehot_done, s + 1)
                    pe.matmul(bank[MISC][0:1, 0:P], const(C_EVEC, 1, n), onehot[:, :], start=True, stop=True)\
                        .then_inc(id_done, 1)
                    pe.wait_ge(ids_done, s + 1)
                    pe.wait_ge(C3_done, s + 1)
                    pe.transpose(bank[MISC][:, 0:P], C3[:, :, :].rearrange("p t n -> p (t n)"), identf[:, :])\
                        .then_inc(C3T_done, 1)
                    pe.wait_ge(C3T_copied, s + 2)
                    for t in range(TPS):
                        rows(2 * TPS * s + (TPS + t), C3T, b2s, t)

            for c in range(NC):
                mm = pe.matmul(bank[MISC][:, c * NR * NE:(c + 1) * NR * NE], pws[:, c, :], uTs[:, :],
                               start=True, stop=True)
            mm.then_inc(M_done, 1)

            by_sequence(step)(pe)

            extras = pe.alloc_register("pe_extras")
            pe.reg_mov(extras, 0)

            def slot(where, lhs, m, e, s):
                k = 0
                for c in range(NC):
                    for hx, hw in ((0, 0), (0, 1), (1, 0)):
                        mm = pe.matmul(where[:, 0:DIM], lhs(hx, c),
                                       W[:, m, bass.ds(e, 1), hw, c * DIM:(c + 1) * DIM].rearrange("p a n -> p (a n)"),
                                       start=(k == 0), stop=(k == 5))
                        k += 1
                mm.then_inc(s, 1)

            def further(flag, lhs, m, t):
                with pe.If(flag != 0):
                    with pe.Fori(1, NREC) as g:
                        v = load_ids(pe, ENGINE.PE, t, m, g)
                        with pe.If(v[0] != 0):
                            n = pe.snap(extras, min_val=0, max_val=2 * NT * NE)
                            for j in range(TOPK):
                                if j != 1:
                                    pe.wait_ge(ex_free, n + (j // 2 + 1))
                                slot(bank[EXTRA[j % 2]], lhs, m, v[j], ex_done)
                            pe.reg_add(extras, extras, TOPK)
                        with pe.Else():
                            pe.nop()
                        pe.nop()
                with pe.Else():
                    pe.nop()
                pe.nop()

            def ffn(t, p, first, second, third):
                if third:
                    u = t - 2
                    v = load_ids(pe, ENGINE.PE, u, 1, 0)
                    pe.wait_ge(hlo_done, u + 2)
                    for j in range(TOPK):
                        if j == 2:
                            further(v[3], lambda hx, c: hT[:, p, hx, c, :], 1, u)
                        pe.wait_ge(m2_free, TOPK * u + (j + 1))
                        slot(bank[MIX2[(TOPK * p + j) % 2]], lambda hx, c: hT[:, p, hx, c, :], 1, v[j], m2_done)
                if second:
                    pe.wait_ge(gelu_done, t)
                    pe.wait_ge(hlo_done, t)
                    for c in range(NC):
                        tr = pe.transpose(bank[HT][:, c * P:(c + 1) * P], hact[:, 1 - p, c * P:(c + 1) * P], identf[:, :])
                    tr.then_inc(hT_done, 1)
                if first:
                    def lhs(hx, c):
                        return x1T[:, bass.ds(t, 1), hx, c, :].rearrange("p a n -> p (a n)")
                    v = load_ids(pe, ENGINE.PE, t, 0, 0)
                    for j in range(TOPK):
                        if j < 2:
                            pe.wait_ge(m1_free, 2 * t + (j + 1))
                        else:
                            further(v[3], lhs, 0, t)
                            pe.wait_ge(m1_init, t + 1)
                        slot(bank[MIX1[(TOPK * p + j) % 2]], lhs, 0, v[j], m1_done)

            pe.wait_ge(w_split, NM * NE)
            pe.wait_ge(row_free, 2 * TPS * NSEQ + 2)
            by_tile(pe, ffn)

        @block.vector
        def _(dve):
            def chain(s, per):
                count = [0, 0]

                def start(base):
                    count[0], count[1] = base, 0

                def link(ins, alone=False):
                    count[1] += 1
                    ins.then_inc(s, 1)
                    (hold if alone else wait)(*((dve, s, count[0] + count[1])))

                def end():
                    assert count[1] == per, count[1]
                return start, link, end

            setup_start, setup, _ = chain(dve_setup, 0)
            setup_start(0)
            attn_start, attn, attn_end = chain(dve_attn, 2)
            route_start, route, route_end = chain(dve_route, 18)

            def rope(b):
                attn_start(2 * b)
                dve.wait_ge(qk_copied, 4 * b + 4)
                if not isinstance(b, int):
                    dve.wait_ge(score_done, TPS * b)
                cos = const(C_COS, SEQ).unsqueeze(1).to_broadcast([P, 4, SEQ])
                sin = const(C_SIN, SEQ).unsqueeze(1).to_broadcast([P, 4, SEQ])
                flat = [a[:, :, :, :].rearrange("p a c n -> p (a c) n") for a in (qk, xcos, xsin)]
                attn(dve.tensor_tensor(flat[1], flat[0], cos, ALU.mult))
                attn(dve.tensor_tensor(flat[2], flat[0], sin, ALU.mult))
                dve.tensor_tensor(qkr[:, :, 0, :], xcos[:, :, 0, :], xsin[:, :, 1, :], ALU.subtract)
                dve.tensor_tensor(qkr[:, :, 1, :], xcos[:, :, 1, :], xsin[:, :, 0, :], ALU.add).then_inc(rope_done, 1)
                attn_end()

            def step(b, attend, do_route):
                s = b - 1
                if do_route:
                    route_start(18 * s)
                    dve.wait_ge(exp_done, TPS * b)
                    sums = o[:, bass.ds((b + 1) % 2, 1), :].rearrange("p a t -> p (a t)")\
                        .unsqueeze(2).to_broadcast([P, TPS, PAD])
                    w, bias = (gatew[:, i, :].unsqueeze(1).to_broadcast([P, TPS, PAD]) for i in (0, 1))
                    route(dve.tensor_tensor(hg[:, :, :], sums, w, ALU.mult))
                    route(dve.tensor_tensor(hg[:, :, :], hg[:, :, :], bias, ALU.add))
                    dve.tensor_scalar(hg[:, :, :], hg[:, :, :], 0.0, None, ALU.max).then_inc(hg_done, 1)
                    for t in range(TPS):
                        xt = xs[:, bass.ds(TPS * s + t, 1), :].rearrange("p a d -> p (a d)")
                        dve.wait_ge(row_done, 2 * TPS * s + (t + 1))
                        dve.tensor_tensor(xt, bank[ROW[t % 2]][:, 0:DIM], xt, ALU.add).then_inc(row_free, 1)
                        hold(dve, row_free, 2 * TPS * s + (t + 3))
                        route(dve.bn_stats(stats[:, t, :], xt), alone=True)
                        dve.bn_aggr(mv[:, t, :], stats[:, t, :]).then_inc(mv_done, 1)
                if attend:
                    rope(b)
                if do_route:
                    dve.wait_ge(mv_done, TPS * s + TPS)
                    dve.wait_ge(rstd_done, s + 1)
                    for t in range(TPS):
                        xt = xs[:, bass.ds(TPS * s + t, 1), :].rearrange("p a d -> p (a d)")
                        dve.tensor_scalar(x1[:, t, :], xt, mv[:, t, 0:1], rstd[:, t:t + 1], ALU.subtract, ALU.mult)\
                            .then_inc(x1_done, 1)
                    for t in range(TPS):
                        dve.wait_ge(x1hi_done, TPS * s + (t + 1))
                        tile = x1T[:, bass.ds(TPS * s + t, 1), :, :, :]
                        dve.tensor_tensor(tile[:, :, 1, :, :].rearrange("p a c n -> p (a c n)"), bank[XPOSE][:, 0:DIM],
                                          tile[:, :, 0, :, :].rearrange("p a c n -> p (a c n)"), ALU.subtract)\
                            .then_inc(x1lo_done, 1)
                    n = TPS * NR
                    dve.wait_ge(z_done, s + 1)
                    dve.tensor_scalar(zs[:, :, :].rearrange("p g e -> p (g e)"), bank[MISC][:, 128:128 + n * NE],
                                      iscale[:, 2:3], None, ALU.mult).then_inc(z_copied, 1)
                    hold(dve, z_copied, s + 1)
                    for g in range(n):
                        mx = dve.max(top8[:, g, :], zs[:, g, :])
                    route(mx, alone=True)
                    for g in range(n):
                        mi = dve.max_index(idx8[:, g, :], top8[:, g, :], zs[:, g, :])
                    route(mi)
                    dve.tensor_tensor(ez[:, :, :], zs[:, :, :], top8[:, :, 0:1].to_broadcast([P, n, NE]), ALU.subtract)\
                        .then_inc(ez_in, 1)
                    lanes = iota12[:, :].unsqueeze(1).to_broadcast([P, n, NE])
                    for j in range(TOPK):
                        pick = dve.tensor_tensor(picked[:, j, :, :], lanes, idx8[:, :, j:j + 1].to_broadcast([P, n, NE]),
                                                 ALU.is_equal)
                    route(pick)
                    route(dve.tensor_tensor(maskf[:, :, :], picked[:, 0, :, :], picked[:, 1, :, :], ALU.add))
                    route(dve.tensor_tensor(maskf[:, :, :], maskf[:, :, :], picked[:, 2, :, :], ALU.add))
                    dve.tensor_copy(maskb[:, :, :, :], maskf[:, :, :].rearrange("p (t r) e -> p t r e", t=TPS)[:, :, 0:NM, :])\
                        .then_inc(mask_done, 1)
                    m = GROUPS * NE
                    dve.wait_ge(count_done, s + 1)
                    route(dve.tensor_scalar(used[:, :], bank[MISC][0:m, 0:1], 1.0, None, ALU.min))
                    dve.tensor_copy(usedb[:, :], used[:, :]).then_inc(used_done, 1)
                    dve.wait_ge(rank_done, s + 1)
                    route(dve.tensor_tensor(rank[:, :], bank[MISC][0:m, 0:1], used[:, :], ALU.mult))
                    dve.tensor_scalar(onehot[:, :], const(C_PICK, GROUPS * NREC * REC, m), rank[:, 0:1], None,
                                      ALU.is_equal).then_inc(onehot_done, 1)
                    dve.wait_ge(ez_done, s + 1)
                    route(dve.tensor_tensor(ez2[:, :, :], ez2[:, :, :], maskf[:, :, :], ALU.mult))
                    route(dve.tensor_reduce(esum[:, :, :].rearrange("p t r -> p (t r)"), ez2[:, :, :], AX.X, ALU.add))
                    route(dve.reciprocal(esum[:, :, :], esum[:, :, :]))
                    route(dve.tensor_tensor(escale[:, :, :], esum[:, :, :],
                                            cscale[:, :].unsqueeze(1).to_broadcast([P, TPS, NR]), ALU.mult))
                    route(dve.tensor_tensor(ez[:, :, :], ez2[:, :, :],
                                            escale[:, :, :].rearrange("p t r -> p (t r)").unsqueeze(2)
                                            .to_broadcast([P, n, NE]), ALU.mult))
                    weights = ez[:, :, :].rearrange("p (t r) e -> p t r e", t=TPS)
                    dve.tensor_copy(C3[:, :, 1:NS], weights[:, :, NM, :]).then_inc(C3_done, 1)
                    dve.wait_ge(id_done, s + 1)
                    dve.tensor_copy(ids[0:1, bass.ds(TPS * s, TPS), :, :, :].rearrange("p t m g r -> p (t m g r)"),
                                    bank[MISC][0:1, 0:P]).then_inc(ids_done, 1)
                    dve.tensor_copy(C[:, bass.ds(TPS * s, TPS), :, 1:NS], weights[:, :, 0:NM, :]).then_inc(C_done, 1)
                    for t in range(TPS):
                        xt = xs[:, bass.ds(TPS * s + t, 1), :].rearrange("p a d -> p (a d)")
                        dve.wait_ge(row_done, 2 * TPS * s + (TPS + t + 1))
                        dve.tensor_tensor(xt, bank[ROW[t % 2]][:, 0:DIM], x1[:, t, :], ALU.add).then_inc(row_free, 1)
                    route_end()

            dve.sem_inc(row_free, 2)
            dve.sem_inc(m1_free, 2)
            dve.sem_inc(m2_free, 2)
            dve.sem_inc(ex_free, 1)
            dve.sem_inc(x1lo_done, 1)
            dve.sem_inc(hlo_done, 1)
            dve.sem_inc(C3T_copied, 1)
            dve.wait_ge(ld_const, 16 * 9)
            step(0, True, False)
            dve.wait_ge(M_done, 1)
            setup(dve.tensor_copy(MTf[:, :, :].rearrange("p c n -> p (c n)"), bank[MISC][:, 0:NC * NR * NE]))
            dve.tensor_reduce(amax[:, 2:3], MTf[:, :, :], AX.XY, ALU.max, apply_absolute_value=True).then_inc(amax_done, 1)
            for m in range(NM):
                dve.wait_ge(ld_w, 16 * (m + 1))
                dve.tensor_reduce(amax[:, m:m + 1], Wf[:, m * NS + 1:(m + 1) * NS, :], AX.XY, ALU.max,
                                  apply_absolute_value=True).then_inc(amax_done, 1)
            dve.wait_ge(amaxa_done, 1)
            setup(dve.tensor_scalar(amaxa[:, :], amaxa[:, :], 1e-30, None, ALU.max))
            setup(dve.tensor_scalar(pow2[:, :].bitcast(U32), amaxa[:, :].bitcast(U32), 0x7F800000, None,
                                    ALU.bitwise_and))
            setup(dve.reciprocal(ipow2[:, :], pow2[:, :]))
            setup(dve.tensor_scalar(scale[:, :], ipow2[:, :], 256.0, None, ALU.mult))
            setup(dve.tensor_scalar(iscale[:, :], pow2[:, :], 1.0 / 256.0, None, ALU.mult))
            setup(dve.memset(cscale[:, :], 1.0))
            setup(dve.tensor_copy(cscale[:, 0:1], iscale[:, 0:1]))
            setup(dve.tensor_tensor(cscale[:, 1:2], iscale[:, 1:2], pow2[:, 0:1], ALU.mult))
            dve.sem_inc(scale_done, 1)
            setup(dve.tensor_scalar(MTf[:, :, :], MTf[:, :, :], scale[:, 2:3], None, ALU.mult))
            setup(dve.tensor_copy(MT[:, 0, :, :], MTf[:, :, :]))
            dve.tensor_tensor(MT[:, 1, :, :], MTf[:, :, :], MT[:, 0, :, :], ALU.subtract).then_inc(MT_done, 1)
            dve.wait_ge(zero_done, 5)
            with dve.Fori(1, NSEQ) as b:
                step(b, True, True)
            step(NSEQ, False, True)

            extras = dve.alloc_register("dve_extras")
            dve.reg_mov(extras, 0)

            def weight(t, m, e):
                return C[:, bass.ds(t, 1), m, bass.ds(e, 1)].rearrange("p a b -> p (a b)")

            def add_slot(sums, where, t, m, e, s):
                dve.scalar_tensor_tensor(sums, where[:, 0:DIM], weight(t, m, e), sums, ALU.mult, ALU.add).then_inc(s, 1)

            def further(flag, sums, t, m):
                with dve.If(flag != 0):
                    with dve.Fori(1, NREC) as g:
                        v = load_ids(dve, ENGINE.DVE, t, m, g)
                        with dve.If(v[0] != 0):
                            n = dve.snap(extras, min_val=0, max_val=2 * NT * NE)
                            for j in range(TOPK):
                                dve.wait_ge(ex_done, n + (j + 1))
                                dve.wait_ge(ex_free, n + (j + 1))
                                add_slot(sums, bank[EXTRA[j % 2]], t, m, v[j], ex_free)
                            dve.reg_add(extras, extras, TOPK)
                        with dve.Else():
                            dve.nop()
                        dve.nop()
                with dve.Else():
                    dve.nop()
                n = dve.snap(extras, min_val=0, max_val=2 * NT * NE)
                hold(dve, ex_free, n + 1)

            def finish(t, p):
                xt = xs[:, bass.ds(t, 1), :].rearrange("p a d -> p (a d)")
                dve.wait_ge(rstd2_done, t + 1)
                dve.wait_ge(mv2_done, t + 1)
                dve.tensor_scalar(xt, xt, mv2[:, p, 0:1], rstd2[:, p:p + 1], ALU.subtract, ALU.mult).then_inc(y_done, 1)

            def ffn(t, p, first, second, third):
                if third:
                    u = t - 2
                    v = load_ids(dve, ENGINE.DVE, u, 1, 0)
                    sums = xs[:, bass.ds(u, 1), :].rearrange("p a d -> p (a d)")
                    for j in range(TOPK):
                        if j:
                            hold(dve, m2_free, TOPK * u + (j + 2))
                        if j == 2:
                            further(v[3], sums, u, 1)
                        dve.wait_ge(m2_done, TOPK * u + (j + 1))
                        add_slot(sums, bank[MIX2[(TOPK * p + j) % 2]], u, 1, v[j], m2_free)
                    hold(dve, m2_free, TOPK * u + 5)
                    dve.bn_stats(st2[:, p, :], sums).then_inc(dve_ffn, 1)
                    hold(dve, dve_ffn, u + 1)
                    dve.bn_aggr(mv2[:, p, :], st2[:, p, :]).then_inc(mv2_done, 1)
                if second:
                    dve.wait_ge(hhi_done, t)
                    dve.scalar_tensor_tensor(hT[:, 1 - p, 1, :, :].rearrange("p c n -> p (c n)"), bank[HT][:, 0:DIM],
                                             ipow2[:, 0:1], hT[:, 1 - p, 0, :, :].rearrange("p c n -> p (c n)"),
                                             ALU.mult, ALU.subtract).then_inc(hlo_done, 1)
                if first:
                    v = load_ids(dve, ENGINE.DVE, t, 0, 0)
                    sums = acc1[:, p, :]
                    dve.wait_ge(m1_init, t + 1)
                    for j in (1, 2):
                        if j == 2:
                            hold(dve, m1_free, 2 * t + 3)
                            further(v[3], sums, t, 0)
                        dve.wait_ge(m1_done, TOPK * t + (j + 1))
                        add_slot(sums, bank[MIX1[(TOPK * p + j) % 2]], t, 0, v[j], m1_free)
                if third:
                    finish(t - 2, p)

            dve.wait_ge(C_done, NSEQ)
            dve.wait_ge(row_free, 2 * TPS * NSEQ + 2)
            by_tile(dve, ffn)


_OUT = (NSEQ, SEQ, DIM)


def kernel(**inputs):
    import ml_dtypes
    import concourse.bacc as _bacc
    from concourse import mybir as _mybir
    from concourse.bass_utils import run_bass_kernel_spmd as _run

    a = {k: np.asarray(v) for k, v in inputs.items()}
    x = a["L0_attn_hidden_states"]
    gate = np.zeros((2, PAD), np.float32)
    gate[0, :INNER] = a["L0_attn_fc1_w"][:, 0]
    gate[1, :INNER] = a["L0_attn_fc1_b"]
    gate[1, INNER] = 1
    fc2 = np.zeros((P // PAD, PAD, DIM), np.float32)
    fc2[:, :INNER] = a["L0_attn_fc2_w"].T
    fc2[:, INNER] = a["L0_attn_fc2_b"]
    b2e = np.zeros((P // PAD, PAD, DIM), np.float32)
    b2e[:, 1:NS] = a["L0_ffn_b2"]
    wqk = np.concatenate([a["L0_attn_Wq"], a["L0_attn_Wk"]]).T.reshape(NC, P, 4, P).transpose(1, 0, 2, 3)

    def experts(w):
        return w.transpose(2, 0, 1).reshape(NC, P, NE, DIM).transpose(1, 2, 0, 3).reshape(P, NE, NC * DIM)

    consts = np.zeros((P, P + NE), np.float32)
    consts[:, :P] = np.eye(P)
    consts[:, P:] = np.arange(NE)
    arrays = {
        "x": x.reshape(NSEQ, TPS, P, DIM),
        "xT": x.reshape(NSEQ, SEQ, NC, P).transpose(0, 3, 2, 1),
        "wqkT": wqk,
        "gate": np.broadcast_to(gate, (P, 2, PAD)),
        "fc2": fc2.reshape(P, DIM),
        "p_w": a["L0_ffn_P_w"],
        "uT": np.concatenate([a["L0_ffn_U1"], a["L0_ffn_U2"], a["L0_ffn_U3"]]).T,
        "w1T": experts(a["L0_ffn_W1"]),
        "w2T": experts(a["L0_ffn_W2"]),
        "b2e": b2e.reshape(P, DIM),
        "constb": shape_constants().astype(ml_dtypes.bfloat16),
        "constf": consts,
    }
    arrays = {"in_" + k: np.ascontiguousarray(v) for k, v in arrays.items()}
    nc = _bacc.Bacc("TRN2", target_bir_lowering=False, num_devices=1)
    args = [nc.dram_tensor(k, v.shape, _mybir.dt.from_np(v.dtype), kind="ExternalInput").ap() for k, v in arrays.items()]
    out = nc.dram_tensor("out", (NT, P, DIM), F32, kind="ExternalOutput").ap()
    build(nc, *args, out)
    r = _run(nc, [arrays], core_ids=[0])
    return r.results[0]["out"].reshape(_OUT)
```

```python
from contextlib import ExitStack

import numpy as np

import concourse.bass as bass
from concourse import mybir

ALU = mybir.AluOpType
ACT = mybir.ActivationFunctionType
AX = mybir.AxisListType
ENGINE = mybir.EngineType
F32 = mybir.dt.float32
F16 = mybir.dt.float16
BF16 = mybir.dt.bfloat16
I32 = mybir.dt.int32
U32 = mybir.dt.uint32

P = 128
DIM = 256
NC = DIM // P
NSEQ, SEQ = 8, 512
TPS = SEQ // P
NT = NSEQ * TPS
INNER = 16
PAD = 32
NE = 12
NS = NE + 1
TOPK = 3
NR = 3
NM = 2
REC = 4
NREC = NE // TOPK
GROUPS = TPS * NM
EPS = 1e-5
MASKED = -1e30
ROPE_BASE = 32.0

C_COS, C_SIN = 0, SEQ
C_IDENT = 2 * SEQ
C_MASK = C_IDENT + P
C_TRI = C_MASK + P
C_PICK = C_TRI + GROUPS * NE
C_EVEC = C_PICK + GROUPS * NREC * REC
C_ONES = C_EVEC + 1
NCONST = C_ONES + 1


def shape_constants():
    half = DIM // 2
    inv = np.float32(ROPE_BASE) ** (-np.arange(0, DIM, 2, dtype=np.float32) / np.float32(DIM))
    ang = np.arange(SEQ, dtype=np.float32)[:, None] * inv.astype(np.float32)
    c = np.zeros((P, NCONST), np.float32)
    assert half == P
    c[:, C_COS:C_COS + SEQ] = np.cos(ang).T
    c[:, C_SIN:C_SIN + SEQ] = np.sin(ang).T
    c[:, C_IDENT:C_IDENT + P] = np.eye(P)
    q, k = np.arange(P)[:, None], np.arange(P)[None, :]
    c[:, C_MASK:C_MASK + P] = np.where(k > q, MASKED, 0.0)
    n = GROUPS * NE
    i, j = np.arange(n)[:, None], np.arange(n)[None, :]
    c[:n, C_TRI:C_TRI + n] = (i // NE == j // NE) & (i <= j)
    place = np.arange(NREC)[:, None] * TOPK + np.arange(REC)[None, :] + 1
    place[place > NE] = -1
    pick = np.full((NM, TPS, NE, TPS, NREC, NM, REC), -1.0, np.float32)
    for t in range(TPS):
        for m in range(NM):
            pick[m, t, :, t, :, m, :] = place
    c[:n, C_PICK:C_PICK + GROUPS * NREC * REC] = pick.reshape(n, -1)
    c[:n, C_EVEC] = np.arange(n) % NE + 1
    c[:, C_ONES] = 1
    return c


def build(nc, x, xT, wqkT, gate, fc2, p_w, uT, w1T, w2T, b2e, constb, constf, out):
    ctx = ExitStack()
    with ctx:
        def sb(name, shape, dt):
            return ctx.enter_context(nc.sbuf_tensor(name, shape, dt))

        def ps(name, shape, dt=F32):
            return ctx.enter_context(nc.psum_tensor(name, shape, dt))

        def sem(name):
            return ctx.enter_context(nc.semaphore(name))

        xs = sb("xs", [P, NT, DIM], F32)
        x1 = sb("x1", [P, TPS, DIM], F32)
        x1T = sb("x1T", [P, NT, 2, NC, P], F16)
        W = sb("W", [P, NM, NS, 2, NC * DIM], F16)
        xTb = sb("xTb", [P, 2, NC, SEQ], F32)
        wqk = sb("wqk", [P, NC, 4, P], F32)
        cb = sb("cb", [P, NCONST], BF16)
        identf = sb("identf", [P, P], F32)
        iota12 = sb("iota12", [P, NE], F32)
        gatew = sb("gatew", [P, 2], F32)
        fc2s = sb("fc2s", [P, DIM], F32)
        b2s = sb("b2s", [P, DIM], F32)
        pws = sb("pws", [64, NC, P], F32)
        uTs = sb("uTs", [64, NR * NE], F32)
        MT = sb("MT", [P, 2, NC, NR * NE], F16)
        MTf = sb("MTf", [P, NC, NR * NE], F32)
        qk = sb("qk", [P, 2, 4, SEQ], BF16)
        xcos = sb("xcos", [P, 2, NC, SEQ], BF16)
        xsin = sb("xsin", [P, 2, NC, SEQ], BF16)
        qkr = sb("qkr", [P, 2, NC, SEQ], BF16)
        expd = sb("expd", [P, 2, SEQ], BF16)
        o = sb("o", [P, 2, TPS], F32)
        hg = sb("hg", [P, TPS, PAD], F32)
        hgT = sb("hgT", [P, P], F32)
        stats = sb("stats", [P, TPS, 6], F32)
        mv = sb("mv", [P, TPS, 2], F32)
        ve = sb("ve", [P, TPS], F32)
        rstd = sb("rstd", [P, TPS], F32)
        nmean = sb("nmean", [P, TPS], F32)
        shift = sb("shift", [P, TPS], F32)
        minus_half = sb("minus_half", [P, TPS], F32)
        zs = sb("zs", [P, NR * TPS, NE], F32)
        top8 = sb("top8", [P, NR * TPS, 8], F32)
        idx8 = sb("idx8", [P, NR * TPS, 8], U32)
        ez = sb("ez", [P, NR * TPS, NE], F32)
        ez2 = sb("ez2", [P, NR * TPS, NE], F32)
        picked = sb("picked", [P, 3, NR * TPS, NE], BF16)
        mask = sb("mask", [P, NR * TPS, NE], BF16)
        esum = sb("esum", [P, NR, TPS], F32)
        escale = sb("escale", [P, NR, TPS], F32)
        C = sb("C", [P, NT, NM, NS], F32)
        C3 = sb("C3", [P, TPS, PAD], F32)
        C3T = sb("C3T", [P, P], F32)
        used = sb("used", [GROUPS * NE, 1], F32)
        usedb = sb("usedb", [GROUPS * NE, 1], BF16)
        rank = sb("rank", [GROUPS * NE, 1], F32)
        onehot = sb("onehot", [GROUPS * NE, GROUPS * NREC * REC], BF16)
        ids = sb("ids", [1, NT, NREC, NM, REC], I32)
        wtmp = sb("wtmp", [P, 2, NC * DIM], F32)
        amax = sb("amax", [P, 3], F32)
        amaxa = sb("amaxa", [P, 3], F32)
        pow2 = sb("pow2", [P, 3], F32)
        ipow2 = sb("ipow2", [P, 3], F32)
        scale = sb("scale", [P, 3], F32)
        iscale = sb("iscale", [P, 3], F32)
        cscale = sb("cscale", [P, NR], F32)
        acc1 = sb("acc1", [P, 2, DIM], F32)
        hact = sb("hact", [P, 2, DIM], F32)
        hT = sb("hT", [P, 2, 2, NC, P], F16)
        st2 = sb("st2", [P, 2, 6], F32)
        mv2 = sb("mv2", [P, 2, 2], F32)
        ve2 = sb("ve2", [P, 2], F32)
        rstd2 = sb("rstd2", [P, 2], F32)

        bank = [ps(f"bank{i}", [P, 512]) for i in range(8)]
        PROJ, SCORE, ROW, XPOSE, MISC = (0, 1), (2, 3), (4, 5), (6, 0), 7
        Z = P
        MIX1, MIX2, EXTRA, HT = (0, 1), (2, 3), (4, 5), 6

        ld_const = sem("ld_const")
        ld_seq = sem("ld_seq")
        ld_w = sem("ld_w")
        proj_done = sem("proj_done")
        qk_copied = sem("qk_copied")
        rope_done = sem("rope_done")
        score_done = sem("score_done")
        exp_done = sem("exp_done")
        hg_done = sem("hg_done")
        hgT_done = sem("hgT_done")
        hgT_copied = sem("hgT_copied")
        fc_done = sem("fc_done")
        fc_added = sem("fc_added")
        bias_done = sem("bias_done")
        bias_added = sem("bias_added")
        mv_done = sem("mv_done")
        rstd_done = sem("rstd_done")
        x1_done = sem("x1_done")
        xs_copied = sem("xs_copied")
        x1T_done = sem("x1T_done")
        x1hi_done = sem("x1hi_done")
        x1lo_done = sem("x1lo_done")
        z_done = sem("z_done")
        z_copied = sem("z_copied")
        ez_in = sem("ez_in")
        ez_done = sem("ez_done")
        mask_done = sem("mask_done")
        count_done = sem("count_done")
        used_done = sem("used_done")
        rank_done = sem("rank_done")
        onehot_done = sem("onehot_done")
        id_done = sem("id_done")
        ids_done = sem("ids_done")
        esum_done = sem("esum_done")
        rank_masked = sem("rank_masked")
        recip_done = sem("recip_done")
        escale_done = sem("escale_done")
        C3_done = sem("C3_done")
        C3T_done = sem("C3T_done")
        C3T_copied = sem("C3T_copied")
        C_done = sem("C_done")
        M_done = sem("M_done")
        MT_done = sem("MT_done")
        amax_done = sem("amax_done")
        amaxa_done = sem("amaxa_done")
        scale_done = sem("scale_done")
        w_split = sem("w_split")
        zero_done = sem("zero_done")
        dve_attn = sem("dve_attn")
        dve_norm = sem("dve_norm")
        dve_route = sem("dve_route")
        dve_setup = sem("dve_setup")
        dve_ffn = sem("dve_ffn")
        pool_step = sem("pool_step")
        m1_done = sem("m1_done")
        m1_init = sem("m1_init")
        m1_free = sem("m1_free")
        m2_done = sem("m2_done")
        m2_free = sem("m2_free")
        ex_done = sem("ex_done")
        ex_free = sem("ex_free")
        gelu_done = sem("gelu_done")
        hT_done = sem("hT_done")
        hhi_done = sem("hhi_done")
        hlo_done = sem("hlo_done")
        mv2_done = sem("mv2_done")
        rstd2_done = sem("rstd2_done")
        y_done = sem("y_done")
        stored = sem("stored")
        held = sem("held")

        Wf = W.rearrange("p m e h n -> p (m e) (h n)").bitcast(F32)

        def const(col, n, rows=P):
            return cb[0:rows, col:col + n]

        def wait(eng, s, value):
            if not (isinstance(value, int) and value <= 0):
                eng.wait_ge(s, value)

        def hold(eng, s, value):
            eng.wait_ge(s, value)
            if not isinstance(value, int):
                eng.sem_inc(held, 1)

        def by_sequence(step, between=lambda i: None):
            for i in range(4):
                step(i, True, i >= 1, i >= 2, i >= 3)
                if i < 3:
                    between(i)

            def run(eng):
                with eng.Fori(4, NSEQ) as i:
                    step(i, True, True, True, True)
                for i in range(NSEQ, NSEQ + 3):
                    step(i, False, i < NSEQ + 1, i < NSEQ + 2, True)
            return run

        def by_tile(step):
            for t in range(NT + 2):
                step(t, t < NT, 1 <= t <= NT, t >= 2)

        def load_ids(engine, t):
            _, v = nc.values_load_multi_w_load_instructions(
                ids[0:1, t, 0, :, :].rearrange("p m r -> p (m r)"), engines=[engine], min_val=0, max_val=NE,
                skip_runtime_bounds_check_because="an id is a sum of one-hot entries times 1..12")
            return v[0:REC], v[REC:2 * REC]

        def further_groups(eng, engine, first, t, m, group):
            def nest(flag, g):
                with eng.If(flag != 0):
                    _, v = nc.values_load_multi_w_load_instructions(
                        ids[0:1, t, g, m, :], engines=[engine], min_val=0, max_val=NE,
                        skip_runtime_bounds_check_because="an id is a sum of one-hot entries times 1..12")
                    group(v)
                    if g + 1 < NREC:
                        nest(v[REC - 1], g + 1)
                    else:
                        eng.nop()
                with eng.Else():
                    eng.nop()
            nest(first[REC - 1], 1)

        block = ctx.enter_context(nc.Block())

        @block.sync
        def _(sp):
            def load_seq(b):
                wait(sp, proj_done, 4 * (b - 1) if not isinstance(b, int) or b > 1 else 0)
                parity = b % 2
                sp.dma_start(xTb[:, bass.ds(parity, 1), :, :].rearrange("p a c n -> p (a c) n"),
                             xT[bass.ds(b, 1), :, :, :].rearrange("a p c n -> p (a c) n")).then_inc(ld_seq, 16)
                sp.dma_start(xs[:, bass.ds(b * TPS, TPS), :],
                             x[bass.ds(b, 1), :, :, :].rearrange("a t p d -> p (a t) d")).then_inc(ld_seq, 16)

            load_seq(0)
            sp.dma_start(pws[:, :, :], p_w.rearrange("k (c p) -> k c p", c=NC)).then_inc(ld_const, 16)
            sp.dma_start(uTs[:, :], uT).then_inc(ld_const, 16)
            sp.dma_start(fc2s[:, :], fc2).then_inc(ld_const, 16)
            sp.dma_start(b2s[:, :], b2e).then_inc(ld_const, 16)
            sp.wait_ge(ld_seq, 32)
            load_seq(1)
            for m, w in ((0, w1T), (1, w2T)):
                sp.dma_start(Wf[:, m * NS + 1:(m + 1) * NS, :], w.rearrange("p e n -> p e n")).then_inc(ld_w, 16)
                sp.wait_ge(ld_w, 16 * (m + 1))
                if m == 0:
                    sp.wait_ge(ld_seq, 64)
                    load_seq(2)
            with sp.Fori(3, NSEQ) as b:
                sp.wait_ge(ld_seq, 32 * b)
                load_seq(b)
            with sp.Fori(0, NT) as t:
                sp.wait_ge(y_done, t + 1)
                sp.dma_start(out[bass.ds(t, 1), :, :].rearrange("a p d -> p (a d)"),
                             xs[:, bass.ds(t, 1), :].rearrange("p a d -> p (a d)")).then_inc(stored, 16)
            sp.wait_ge(stored, 16 * NT)

        @block.gpsimd
        def _(pool):
            steps = [0]

            def link(ins):
                steps[0] += 1
                ins.then_inc(pool_step, 1)
                pool.wait_ge(pool_step, steps[0])

            pool.memset(minus_half[:, :], -0.5).then_inc(zero_done, 1)
            pool.memset(C[:, :, :, 0:1], 0.0).then_inc(zero_done, 1)
            pool.memset(C3[:, :, :], 0.0).then_inc(zero_done, 1)
            for m in range(NM):
                pool.memset(Wf[:, m * NS, :], 0.0).then_inc(zero_done, 1)
            pool.wait_ge(zero_done, 5)

            def norm(s):
                pool.wait_ge(mv_done, s + 1)
                if s:
                    pool.wait_ge(x1_done, 2 * s)
                link(pool.tensor_scalar(ve[:, :], mv[:, :, 1], EPS, 0.0, ALU.add, ALU.add))
                link(pool.tensor_tensor(rstd[:, :], ve[:, :], minus_half[:, :], ALU.pow))
                link(pool.tensor_scalar(nmean[:, :], mv[:, :, 0], -1.0, 0.0, ALU.mult, ALU.add))
                pool.tensor_tensor(shift[:, :], nmean[:, :], rstd[:, :], ALU.mult).then_inc(rstd_done, 1)

            norm(0)
            pool.wait_ge(amax_done, 3)
            pool.partition_all_reduce(amaxa[:, :], amax[:, :], P, bass.bass_isa.ReduceOp.max).then_inc(amaxa_done, 1)
            pool.wait_ge(scale_done, 1)
            pieces = [(m, e) for m in range(NM) for e in range(1, NS)]
            per = len(pieces) // NSEQ
            for s in range(NSEQ):
                if s:
                    norm(s)
                for i, (m, e) in enumerate(pieces[s * per:(s + 1) * per]):
                    tmp = wtmp[:, i % 2, :]
                    link(pool.tensor_scalar(tmp, Wf[:, m * NS + e, :], scale[:, m:m + 1], 0.0, ALU.mult, ALU.add))
                    link(pool.tensor_copy(W[:, m, e, 0, :], tmp))
                    pool.tensor_tensor(W[:, m, e, 1, :], tmp, W[:, m, e, 0, :], ALU.subtract).then_inc(w_split, 1)
            base = steps[0]
            with pool.Fori(0, NT, 2) as t:
                for p in range(2):
                    hold(pool, mv2_done, t + p + 1)
                    pool.tensor_scalar(ve2[:, p:p + 1], mv2[:, p, 1:2], EPS, 0.0, ALU.add, ALU.add)\
                        .then_inc(pool_step, 1)
                    pool.wait_ge(pool_step, t + (base + p + 1))
                    pool.tensor_tensor(rstd2[:, p:p + 1], ve2[:, p:p + 1], minus_half[:, 0:1], ALU.pow)\
                        .then_inc(rstd2_done, 1)

        @block.scalar
        def _(act):
            act.dma_start(wqk[:, :, :, :], wqkT).then_inc(ld_const, 16)
            act.dma_start(cb[:, :], constb).then_inc(ld_const, 16)
            act.dma_start(identf[:, :], constf[:, 0:P]).then_inc(ld_const, 16)
            act.dma_start(iota12[:, :], constf[:, P:P + NE]).then_inc(ld_const, 16)
            act.dma_start(gatew[:, :], gate).then_inc(ld_const, 16)

            def step(i, project, attend, norm, route):
                j, a, s = i - 1, i - 2, i - 3

                def copy_qk(g):
                    act.wait_ge(proj_done, 4 * i + (g + 1))
                    act.activation(qk[:, bass.ds(i % 2, 1), g, :].rearrange("p a n -> p (a n)"), bank[PROJ[g % 2]][:, :],
                                   ACT.Copy).then_inc(qk_copied, 1)

                if norm:
                    act.wait_ge(hgT_done, a + 1)
                    act.activation(hgT[:, :], bank[XPOSE[0]][:, 0:P], ACT.Relu, bias=gatew[:, 1:2],
                                   scale=gatew[:, 0:1]).then_inc(hgT_copied, 1)
                if project:
                    if norm:
                        act.wait_ge(rope_done, i - 1)
                    copy_qk(0)
                    copy_qk(1)
                if attend:
                    if norm and (route or j >= 2):
                        act.wait_ge(hg_done, j - 1)
                    for t in range(TPS):
                        act.wait_ge(score_done, TPS * j + (t + 1))
                        n = (t + 1) * P
                        act.activation(expd[:, t % 2, 0:n], bank[SCORE[t % 2]][:, 0:n], ACT.Exp, scale=float(DIM) ** -0.5,
                                       accum_out=o[:, bass.ds((i + 1) % 2, 1), t]).then_inc(exp_done, 1)
                if route:
                    act.wait_ge(ez_in, s + 1)
                    act.activation(ez2[:, :, :], ez[:, :, :], ACT.Exp).then_inc(ez_done, 1)
                if project:
                    copy_qk(2)
                    copy_qk(3)
                if norm:
                    act.wait_ge(rstd_done, a + 1)
                    if route:
                        act.wait_ge(xs_copied, a)
                    for t in range(TPS):
                        x1t = act.activation(x1[:, t, :], xs[:, bass.ds(TPS * a + t, 1), :].rearrange("p a d -> p (a d)"),
                                             ACT.Identity, bias=shift[:, t:t + 1], scale=rstd[:, t:t + 1])
                        if t % 2:
                            x1t.then_inc(x1_done, 1)
                    for h in range(2):
                        act.wait_ge(x1T_done, 2 * a + (h + 1))
                        act.activation(x1T[:, bass.ds(TPS * a + 2 * h, 2), 0, :, :].rearrange("p t c n -> p t (c n)"),
                                       bank[XPOSE[h]][:, :].rearrange("p (t n) -> p t n", t=2), ACT.Copy)\
                            .then_inc(x1hi_done, 1)
                if route:
                    act.wait_ge(C3T_done, s + 1)
                    act.activation(C3T[:, :], bank[MISC][:, 0:P], ACT.Copy).then_inc(C3T_copied, 1)
                if norm:
                    hold(act, x1_done, 2 * (a + 1))
                    act.activation(xs[:, bass.ds(TPS * a, TPS), :], x1[:, :, :], ACT.Copy).then_inc(xs_copied, 1)

            by_sequence(step)(act)

            def ffn(t, first, second, third):
                p = t % 2
                if second:
                    act.wait_ge(hT_done, t)
                    act.activation(hT[:, 1 - p, 0, :, :].rearrange("p c n -> p (c n)"), bank[HT][:, 0:DIM], ACT.Copy,
                                   scale=ipow2[:, 0:1]).then_inc(hhi_done, 1)
                if first:
                    v, _ = load_ids(ENGINE.Activation, t)
                    act.wait_ge(m1_done, TOPK * t + 1)
                    b = MIX1[(TOPK * p) % 2]
                    act.activation(acc1[:, p, :], bank[b][:, 0:DIM], ACT.Copy,
                                   scale=C[:, t, 0, bass.ds(v[0], 1)])\
                        .then_inc(m1_init, 1)
                    act.wait_ge(m1_free, 2 * t + 4)
                    act.activation(hact[:, p, :], acc1[:, p, :], ACT.Gelu).then_inc(gelu_done, 1)

            act.wait_ge(ids_done, NSEQ)
            act.wait_ge(C_done, NSEQ)
            by_tile(ffn)

        @block.tensor
        def _(pe):
            pe.wait_ge(ld_const, 16 * 9)
            pe.wait_ge(ld_seq, 32)

            def step(i, project, attend, norm, route):
                j, a, s = i - 1, i - 2, i - 3

                def features(g):
                    if g == 0:
                        pe.wait_ge(ld_seq, 32 * i + 32)
                        if route:
                            pe.wait_ge(x1lo_done, 2 * (s + 1))
                    if attend or g >= 2:
                        pe.wait_ge(qk_copied, 4 * i + (g - 1))
                    for c in range(NC):
                        mm = pe.matmul(bank[PROJ[g % 2]][:, :], wqk[:, c, g, :],
                                       xTb[:, bass.ds(i % 2, 1), c, :].rearrange("p a n -> p (a n)"),
                                       start=(c == 0), stop=(c == NC - 1))
                    mm.then_inc(proj_done, 1)

                def rows(n, lhsT, rhs, done):
                    for t in range(TPS):
                        lo, hi = PAD * t, PAD * (t + 1)
                        if t >= 2:
                            pe.wait_ge(done, TPS * n + (t - 1))
                        pe.matmul(bank[ROW[t % 2]][:, t // 2 * DIM:(t // 2 + 1) * DIM], lhsT[lo:hi, :], rhs[lo:hi, :],
                                  start=True, stop=True).then_inc(done, 1)

                if norm:
                    pe.wait_ge(hg_done, a + 1)
                    if route:
                        pe.wait_ge(x1lo_done, 2 * a)
                    pe.transpose(bank[XPOSE[0]][:, 0:P], hg[:, :, :].rearrange("p t n -> p (t n)"), identf[:, :])\
                        .then_inc(hgT_done, 1)
                if route:
                    pe.wait_ge(MT_done, 1)
                    pe.wait_ge(x1lo_done, 2 * (s + 1))
                    for t in range(TPS):
                        zr = bank[MISC][:, Z + t * NR * NE:Z + (t + 1) * NR * NE]
                        k = 0
                        for c in range(NC):
                            for hx, hm in ((0, 0), (0, 1), (1, 0)):
                                mm = pe.matmul(zr, x1T[:, bass.ds(TPS * s + t, 1), hx, c, :].rearrange("p a n -> p (a n)"),
                                               MT[:, hm, c, :], start=(k == 0), stop=(k == 5))
                                k += 1
                    mm.then_inc(z_done, 1)
                if project:
                    features(0)
                    features(1)
                if norm:
                    pe.wait_ge(hgT_copied, a + 1)
                    pe.wait_ge(bias_added, 2 * a + 2)
                    rows(a, hgT, fc2s, fc_done)
                if attend:
                    pe.wait_ge(rope_done, i)
                    for t in range(TPS):
                        if norm or t >= 2:
                            pe.wait_ge(exp_done, TPS * j + (t - 1))
                        n = (t + 1) * P
                        sc = bank[SCORE[t % 2]]
                        for c in range(NC):
                            pe.matmul(sc[:, 0:n], qkr[:, 0, c, t * P:(t + 1) * P], qkr[:, 1, c, 0:n],
                                      start=(c == 0), stop=False, skip_group_check=True)
                        pe.matmul(sc[:, t * P:n], const(C_IDENT, P), const(C_MASK, P),
                                  start=False, stop=True, skip_group_check=True).then_inc(score_done, 1)
                n = GROUPS * NE
                if route:
                    pe.wait_ge(mask_done, s + 1)
                    pe.matmul(bank[MISC][0:n, 0:1], mask[:, 0:GROUPS, :].rearrange("p g e -> p (g e)"),
                              const(C_ONES, 1), start=True, stop=True).then_inc(count_done, 1)
                if project:
                    features(2)
                    features(3)
                if route:
                    pe.wait_ge(used_done, s + 1)
                    pe.matmul(bank[MISC][0:n, 0:1], const(C_TRI, n, n), usedb[:, :], start=True, stop=True)\
                        .then_inc(rank_done, 1)
                    pe.wait_ge(onehot_done, s + 1)
                    pe.matmul(bank[MISC][0:1, 0:P], const(C_EVEC, 1, n), onehot[:, :], start=True, stop=True)\
                        .then_inc(id_done, 1)
                if norm:
                    for h in range(2):
                        pe.wait_ge(x1_done, 2 * a + (h + 1))
                        if h and project:
                            pe.wait_ge(qk_copied, 4 * i + 3)
                        for t in range(2):
                            for c in range(NC):
                                tr = pe.transpose(bank[XPOSE[h]][:, t * DIM + c * P:t * DIM + (c + 1) * P],
                                                  x1[:, 2 * h + t, c * P:(c + 1) * P], identf[:, :])
                        tr.then_inc(x1T_done, 1)
                if route:
                    pe.wait_ge(C3_done, s + 1)
                    pe.wait_ge(ids_done, s + 1)
                    pe.transpose(bank[MISC][:, 0:P], C3[:, :, :].rearrange("p t n -> p (t n)"), identf[:, :])\
                        .then_inc(C3T_done, 1)
                    pe.wait_ge(C3T_copied, s + 1)
                    pe.wait_ge(fc_added, 2 * (s + 2) if norm else 2 * NSEQ)
                    rows(s, C3T, b2s, bias_done)

            for c in range(NC):
                mm = pe.matmul(bank[MISC][:, c * NR * NE:(c + 1) * NR * NE], pws[:, c, :], uTs[:, :],
                               start=True, stop=True)
            mm.then_inc(M_done, 1)

            by_sequence(step)(pe)

            extras = pe.alloc_register("pe_extras")
            pe.reg_mov(extras, 0)

            def slot(where, lhs, m, e, s):
                k = 0
                for c in range(NC):
                    for hx, hw in ((0, 0), (0, 1), (1, 0)):
                        mm = pe.matmul(where[:, 0:DIM], lhs(hx, c),
                                       W[:, m, bass.ds(e, 1), hw, c * DIM:(c + 1) * DIM].rearrange("p a n -> p (a n)"),
                                       start=(k == 0), stop=(k == 5))
                        k += 1
                mm.then_inc(s, 1)

            def further(first, lhs, m, t):
                def group(v):
                    n = pe.snap(extras, min_val=0, max_val=2 * NT * NE)
                    for j in range(TOPK):
                        if j != 1:
                            pe.wait_ge(ex_free, n + (j // 2 + 1))
                        slot(bank[EXTRA[j % 2]], lhs, m, v[j], ex_done)
                    pe.reg_add(extras, extras, TOPK)
                further_groups(pe, ENGINE.PE, first, t, m, group)

            loaded = {}

            def ffn(t, first, second, third):
                p = t % 2
                if first:
                    loaded[t] = load_ids(ENGINE.PE, t)
                if third:
                    u = t - 2
                    v = loaded.pop(u)[1]
                    pe.wait_ge(hlo_done, u + 2)
                    for j in range(TOPK):
                        if j == 2:
                            further(v, lambda hx, c: hT[:, p, hx, c, :], 1, u)
                        pe.wait_ge(m2_free, TOPK * u + (j + 1))
                        slot(bank[MIX2[(TOPK * p + j) % 2]], lambda hx, c: hT[:, p, hx, c, :], 1, v[j], m2_done)
                if second:
                    pe.wait_ge(gelu_done, t)
                    pe.wait_ge(hlo_done, t)
                    for c in range(NC):
                        tr = pe.transpose(bank[HT][:, c * P:(c + 1) * P], hact[:, 1 - p, c * P:(c + 1) * P], identf[:, :])
                    tr.then_inc(hT_done, 1)
                if first:
                    v = loaded[t][0]
                    for j in range(TOPK):
                        if j < 2:
                            pe.wait_ge(m1_free, 2 * t + (j + 1))
                        else:
                            further(v, lambda hx, c: x1T[:, t, hx, c, :], 0, t)
                            pe.wait_ge(m1_init, t + 1)
                        slot(bank[MIX1[(TOPK * p + j) % 2]], lambda hx, c: x1T[:, t, hx, c, :], 0, v[j], m1_done)

            pe.wait_ge(w_split, NM * NE)
            pe.wait_ge(bias_added, 2 * NSEQ + 4)
            by_tile(ffn)

        @block.vector
        def _(dve):
            def chain(s, per):
                count = [0, 0]

                def start(base):
                    count[0], count[1] = base, 0

                def link(ins, alone=False):
                    count[1] += 1
                    ins.then_inc(s, 1)
                    (hold if alone else wait)(*((dve, s, count[0] + count[1])))

                def end():
                    assert count[1] == per, count[1]
                return start, link, end

            setup_start, setup, _ = chain(dve_setup, 0)
            setup_start(0)
            attn_start, attn, attn_end = chain(dve_attn, 2)
            norm_start, norm_link, norm_end = chain(dve_norm, 1)
            route_start, route, route_end = chain(dve_route, 6)

            def rope(b):
                attn_start(2 * b)
                dve.wait_ge(qk_copied, 4 * b + 4)
                if not isinstance(b, int) or b > 0:
                    dve.wait_ge(score_done, TPS * b)
                cos = const(C_COS, SEQ).unsqueeze(1).to_broadcast([P, 4, SEQ])
                sin = const(C_SIN, SEQ).unsqueeze(1).to_broadcast([P, 4, SEQ])
                flat = [qk[:, bass.ds(b % 2, 1), :, :].rearrange("p a c n -> p (a c) n")]
                flat += [a[:, :, :, :].rearrange("p a c n -> p (a c) n") for a in (xcos, xsin)]
                attn(dve.tensor_tensor(flat[1], flat[0], cos, ALU.mult))
                attn(dve.tensor_tensor(flat[2], flat[0], sin, ALU.mult))
                dve.tensor_tensor(qkr[:, :, 0, :], xcos[:, :, 0, :], xsin[:, :, 1, :], ALU.subtract)
                dve.tensor_tensor(qkr[:, :, 1, :], xcos[:, :, 1, :], xsin[:, :, 0, :], ALU.add).then_inc(rope_done, 1)
                attn_end()

            def row_add(i, done, added):
                for h in range(2):
                    tiles = xs[:, bass.ds(TPS * i, TPS), :].rearrange("p (u v) d -> p v u d", v=2)[:, h, :, :]
                    dve.wait_ge(done, TPS * i + (h + 3))
                    dve.tensor_tensor(tiles, bank[ROW[h]][:, :].rearrange("p (u d) -> p u d", u=2), tiles, ALU.add)\
                        .then_inc(added, 1)

            def add_bias(s):
                dve.wait_ge(xs_copied, s + 1)
                row_add(s, bias_done, bias_added)

            def step(i, project, attend, norm, do_route):
                a, s = i - 2, i - 3
                n, m = NR * TPS, GROUPS * NE
                if norm:
                    norm_start(a)
                    dve.wait_ge(exp_done, TPS * (a + 1))
                    dve.tensor_copy(hg[:, :, :], o[:, bass.ds(i % 2, 1), :].rearrange("p a t -> p (a t)")
                                    .unsqueeze(2).to_broadcast([P, TPS, PAD])).then_inc(hg_done, 1)
                if attend:
                    rope(i - 1)
                if not isinstance(i, int) or i >= 4:
                    add_bias(s - 1)
                if do_route:
                    route_start(6 * s)
                    dve.wait_ge(z_done, s + 1)
                    dve.tensor_scalar(zs[:, :, :].rearrange("p (r t) e -> p t r e", r=NR),
                                      bank[MISC][:, Z:Z + n * NE].rearrange("p (t r e) -> p t r e", t=TPS, r=NR),
                                      iscale[:, 2:3], None, ALU.mult).then_inc(z_copied, 1)
                    hold(dve, z_copied, s + 1)
                    for g in range(n):
                        mx = dve.max(top8[:, g, :], zs[:, g, :])
                    route(mx, alone=True)
                    for g in range(n):
                        mi = dve.max_index(idx8[:, g, :], top8[:, g, :], zs[:, g, :])
                    route(mi)
                    dve.tensor_tensor(ez[:, :, :], zs[:, :, :], top8[:, :, 0:1].to_broadcast([P, n, NE]), ALU.subtract)\
                        .then_inc(ez_in, 1)
                    lanes = iota12[:, :].unsqueeze(1).to_broadcast([P, n, NE])
                    for j in range(TOPK):
                        pick = dve.tensor_tensor(picked[:, j, :, :], lanes, idx8[:, :, j:j + 1].to_broadcast([P, n, NE]),
                                                 ALU.is_equal)
                    route(pick)
                    route(dve.tensor_tensor(mask[:, :, :], picked[:, 0, :, :], picked[:, 1, :, :], ALU.add))
                    dve.tensor_tensor(mask[:, :, :], mask[:, :, :], picked[:, 2, :, :], ALU.add).then_inc(mask_done, 1)
                if norm:
                    row_add(a, fc_done, fc_added)
                    hold(dve, fc_added, 2 * (a + 1))
                    for t in range(TPS):
                        xt = xs[:, bass.ds(TPS * a + t, 1), :].rearrange("p a d -> p (a d)")
                        st = dve.bn_stats(stats[:, t, :], xt)
                    norm_link(st, alone=True)
                    for t in range(TPS):
                        ag = dve.bn_aggr(mv[:, t, :], stats[:, t, :])
                    ag.then_inc(mv_done, 1)
                    norm_end()
                if do_route:
                    dve.wait_ge(count_done, s + 1)
                    route(dve.tensor_scalar(used[:, :], bank[MISC][0:m, 0:1], 1.0, None, ALU.min))
                    dve.tensor_copy(usedb[:, :], used[:, :]).then_inc(used_done, 1)
                    dve.wait_ge(ez_done, s + 1)
                    dve.wait_ge(mask_done, s + 1)
                    route(dve.tensor_tensor(ez2[:, :, :], ez2[:, :, :], mask[:, :, :], ALU.mult))
                    dve.tensor_reduce(esum[:, :, :].rearrange("p r t -> p (r t)"), ez2[:, :, :], AX.X, ALU.add)\
                        .then_inc(esum_done, 1)
                    dve.wait_ge(rank_done, s + 1)
                    dve.tensor_tensor(rank[:, :], bank[MISC][0:m, 0:1], used[:, :], ALU.mult)\
                        .then_inc(rank_masked, 1)
                    dve.wait_ge(esum_done, s + 1)
                    dve.reciprocal(esum[:, :, :], esum[:, :, :]).then_inc(recip_done, 1)
                    dve.wait_ge(rank_masked, s + 1)
                    dve.tensor_scalar(onehot[:, :], const(C_PICK, GROUPS * NREC * REC, m), rank[:, 0:1], None,
                                      ALU.is_equal).then_inc(onehot_done, 1)
                    dve.wait_ge(recip_done, s + 1)
                    dve.tensor_tensor(escale[:, :, :], esum[:, :, :], cscale[:, :].unsqueeze(2).to_broadcast([P, NR, TPS]),
                                      ALU.mult).then_inc(escale_done, 1)
                if do_route:
                    dve.wait_ge(escale_done, s + 1)
                    weights = ez2[:, :, :].rearrange("p (r t) e -> p t r e", r=NR)
                    scales = escale[:, :, :].rearrange("p r t -> p t r").unsqueeze(3).to_broadcast([P, TPS, NR, NE])
                    dve.tensor_tensor(C3[:, :, 1:NS], weights[:, :, NM, :], scales[:, :, NM, :], ALU.mult)\
                        .then_inc(C3_done, 1)
                    for k in range(NM):
                        ck = dve.tensor_tensor(C[:, bass.ds(TPS * s, TPS), k, 1:NS], weights[:, :, k, :],
                                               scales[:, :, k, :], ALU.mult)
                    ck.then_inc(C_done, 1)
                    dve.wait_ge(id_done, s + 1)
                    dve.tensor_copy(ids[0:1, bass.ds(TPS * s, TPS), :, :, :].rearrange("p t g m r -> p (t g m r)"),
                                    bank[MISC][0:1, 0:P]).then_inc(ids_done, 1)
                if norm:
                    for h in range(2):
                        dve.wait_ge(x1hi_done, 2 * a + (h + 1))
                        tiles = x1T[:, bass.ds(TPS * a + 2 * h, 2), :, :, :].rearrange("p t l c n -> p t l (c n)")
                        dve.tensor_tensor(tiles[:, :, 1, :], bank[XPOSE[h]][:, :].rearrange("p (t n) -> p t n", t=2),
                                          tiles[:, :, 0, :], ALU.subtract).then_inc(x1lo_done, 1)
                if do_route:
                    route_end()

            dve.sem_inc(bias_added, 4)
            dve.sem_inc(m1_free, 2)
            dve.sem_inc(m2_free, 2)
            dve.sem_inc(ex_free, 1)
            dve.sem_inc(hlo_done, 1)
            dve.wait_ge(ld_const, 16 * 9)

            def between(i):
                if i == 0:
                    dve.wait_ge(M_done, 1)
                    setup(dve.tensor_copy(MTf[:, :, :].rearrange("p c n -> p (c n)"), bank[MISC][:, 0:NC * NR * NE]))
                    dve.tensor_reduce(amax[:, 2:3], MTf[:, :, :], AX.XY, ALU.max, apply_absolute_value=True)\
                        .then_inc(amax_done, 1)
                else:
                    m = i - 1
                    dve.wait_ge(ld_w, 16 * (m + 1))
                    dve.tensor_reduce(amax[:, m:m + 1], Wf[:, m * NS + 1:(m + 1) * NS, :], AX.XY, ALU.max,
                                      apply_absolute_value=True).then_inc(amax_done, 1)
                if i == 2:
                    set_scales()

            def set_scales():
                dve.wait_ge(amaxa_done, 1)
                setup(dve.tensor_scalar(amaxa[:, :], amaxa[:, :], 1e-30, None, ALU.max))
                setup(dve.tensor_scalar(pow2[:, :].bitcast(U32), amaxa[:, :].bitcast(U32), 0x7F800000, None,
                                        ALU.bitwise_and))
                setup(dve.reciprocal(ipow2[:, :], pow2[:, :]))
                setup(dve.tensor_scalar(scale[:, :], ipow2[:, :], 256.0, None, ALU.mult))
                setup(dve.tensor_scalar(iscale[:, :], pow2[:, :], 1.0 / 256.0, None, ALU.mult))
                setup(dve.memset(cscale[:, :], 1.0))
                setup(dve.tensor_copy(cscale[:, 0:1], iscale[:, 0:1]))
                setup(dve.tensor_tensor(cscale[:, 1:2], iscale[:, 1:2], pow2[:, 0:1], ALU.mult))
                dve.sem_inc(scale_done, 1)
                setup(dve.tensor_scalar(MTf[:, :, :], MTf[:, :, :], scale[:, 2:3], None, ALU.mult))
                setup(dve.tensor_copy(MT[:, 0, :, :], MTf[:, :, :]))
                dve.tensor_tensor(MT[:, 1, :, :], MTf[:, :, :], MT[:, 0, :, :], ALU.subtract).then_inc(MT_done, 1)
                dve.wait_ge(zero_done, 5)

            by_sequence(step, between)(dve)
            add_bias(NSEQ - 1)

            extras = dve.alloc_register("dve_extras")
            dve.reg_mov(extras, 0)

            def add_slot(sums, where, t, m, e, s):
                dve.scalar_tensor_tensor(sums, where[:, 0:DIM], C[:, t, m, bass.ds(e, 1)], sums, ALU.mult, ALU.add)\
                    .then_inc(s, 1)

            def further(first, sums, t, m):
                def group(v):
                    n = dve.snap(extras, min_val=0, max_val=2 * NT * NE)
                    for j in range(TOPK):
                        dve.wait_ge(ex_done, n + (j + 1))
                        dve.wait_ge(ex_free, n + (j + 1))
                        add_slot(sums, bank[EXTRA[j % 2]], t, m, v[j], ex_free)
                    hold(dve, ex_free, n + (TOPK + 1))
                    dve.reg_add(extras, extras, TOPK)
                further_groups(dve, ENGINE.DVE, first, t, m, group)

            loaded = {}

            def ffn(t, first, second, third):
                p = t % 2
                if first:
                    loaded[t] = load_ids(ENGINE.DVE, t)
                if third:
                    u = t - 2
                    v = loaded.pop(u)[1]
                    sums = xs[:, u, :]
                    for j in range(TOPK):
                        if j:
                            dve.wait_ge(m2_free, TOPK * u + (j + 2))
                        if j == 2:
                            further(v, sums, u, 1)
                        dve.wait_ge(m2_done, TOPK * u + (j + 1))
                        add_slot(sums, bank[MIX2[(TOPK * p + j) % 2]], u, 1, v[j], m2_free)
                    dve.wait_ge(m2_free, TOPK * u + 5)
                    dve.bn_stats(st2[:, p, :], sums).then_inc(dve_ffn, 1)
                    dve.wait_ge(dve_ffn, u + 1)
                    dve.bn_aggr(mv2[:, p, :], st2[:, p, :]).then_inc(mv2_done, 1)
                if second:
                    dve.wait_ge(hhi_done, t)
                    dve.scalar_tensor_tensor(hT[:, 1 - p, 1, :, :].rearrange("p c n -> p (c n)"), bank[HT][:, 0:DIM],
                                             ipow2[:, 0:1], hT[:, 1 - p, 0, :, :].rearrange("p c n -> p (c n)"),
                                             ALU.mult, ALU.subtract).then_inc(hlo_done, 1)
                if first:
                    v = loaded[t][0]
                    sums = acc1[:, p, :]
                    dve.wait_ge(m1_init, t + 1)
                    for j in (1, 2):
                        if j == 2:
                            dve.wait_ge(m1_free, 2 * t + 3)
                            further(v, sums, t, 0)
                        dve.wait_ge(m1_done, TOPK * t + (j + 1))
                        add_slot(sums, bank[MIX1[(TOPK * p + j) % 2]], t, 0, v[j], m1_free)
                if third:
                    dve.wait_ge(rstd2_done, u + 1)
                    dve.wait_ge(mv2_done, u + 1)
                    dve.tensor_scalar(xs[:, u, :], xs[:, u, :], mv2[:, p, 0:1], rstd2[:, p:p + 1], ALU.subtract, ALU.mult)\
                        .then_inc(y_done, 1)

            dve.wait_ge(C_done, NSEQ)
            dve.wait_ge(bias_added, 2 * NSEQ + 4)
            by_tile(ffn)


_OUT = (NSEQ, SEQ, DIM)


def kernel(**inputs):
    import ml_dtypes
    import concourse.bacc as _bacc
    from concourse import mybir as _mybir
    from concourse.bass_utils import run_bass_kernel_spmd as _run

    a = {k: np.asarray(v) for k, v in inputs.items()}
    x = a["L0_attn_hidden_states"]
    gate = np.zeros((P // PAD, PAD, 2), np.float32)
    gate[:, :INNER, 0] = a["L0_attn_fc1_w"][:, 0]
    gate[:, :INNER, 1] = a["L0_attn_fc1_b"]
    gate[:, INNER, 1] = 1
    fc2 = np.zeros((P // PAD, PAD, DIM), np.float32)
    fc2[:, :INNER] = a["L0_attn_fc2_w"].T
    fc2[:, INNER] = a["L0_attn_fc2_b"]
    b2e = np.zeros((P // PAD, PAD, DIM), np.float32)
    b2e[:, 1:NS] = a["L0_ffn_b2"]
    wqk = np.concatenate([a["L0_attn_Wq"], a["L0_attn_Wk"]]).T.reshape(NC, P, 4, P).transpose(1, 0, 2, 3)

    def experts(w):
        return w.transpose(2, 0, 1).reshape(NC, P, NE, DIM).transpose(1, 2, 0, 3).reshape(P, NE, NC * DIM)

    consts = np.zeros((P, P + NE), np.float32)
    consts[:, :P] = np.eye(P)
    consts[:, P:] = np.arange(NE)
    arrays = {
        "x": x.reshape(NSEQ, TPS, P, DIM),
        "xT": x.reshape(NSEQ, SEQ, NC, P).transpose(0, 3, 2, 1),
        "wqkT": wqk,
        "gate": gate.reshape(P, 2),
        "fc2": fc2.reshape(P, DIM),
        "p_w": a["L0_ffn_P_w"],
        "uT": np.concatenate([a["L0_ffn_U1"], a["L0_ffn_U2"], a["L0_ffn_U3"]]).T,
        "w1T": experts(a["L0_ffn_W1"]),
        "w2T": experts(a["L0_ffn_W2"]),
        "b2e": b2e.reshape(P, DIM),
        "constb": shape_constants().astype(ml_dtypes.bfloat16),
        "constf": consts,
    }
    arrays = {"in_" + k: np.ascontiguousarray(v) for k, v in arrays.items()}
    nc = _bacc.Bacc("TRN2", target_bir_lowering=False, num_devices=1)
    args = [nc.dram_tensor(k, v.shape, _mybir.dt.from_np(v.dtype), kind="ExternalInput").ap() for k, v in arrays.items()]
    out = nc.dram_tensor("out", (NT, P, DIM), F32, kind="ExternalOutput").ap()
    build(nc, *args, out)
    r = _run(nc, [arrays], core_ids=[0])
    return r.results[0]["out"].reshape(_OUT)
```
